# Optimizing a Trainium2 kernel written in Bass

```python
import numpy as np
import jax
import jax.numpy as jnp

def _softmax(x, axis=-1):
    return jax.nn.softmax(x, axis=axis)

def _gelu(x):
    return jax.nn.gelu(x, approximate=True)

def _silu(x):
    return jax.nn.silu(x)

def _sigmoid(x):
    return jax.nn.sigmoid(x)

def _layernorm(x, axis=-1, eps=1e-05):
    m = jnp.mean(x, axis=axis, keepdims=True)
    v = jnp.var(x, axis=axis, keepdims=True)
    return (x - m) / jnp.sqrt(v + eps)

def _scatter_add(tgt, idx, src, axis=0):
    return tgt.at[idx].add(src)

def _segment_sum(src, seg, n):
    return jax.ops.segment_sum(src, seg, n)
kernel_name = 'mk_macaron_d1_jaxref_r8_6b26a0'

def setup_inputs(seed: int=0):
    np.random.seed(seed)
    _w = jnp.asarray

    def _L0_attn_setup():
        import jax, jax.numpy as jnp
        import numpy as np
        HEADS = 8
        BLOCK = 32
        key = jax.random.key(seed)
        ks = jax.random.split(key, 4)
        b, n, d, f = (4, 512, 128, 128)
        x = jax.random.normal(ks[0], (b, n, d), dtype=jnp.float32)
        w_qkv = jax.random.normal(ks[1], (3 * d, d), dtype=jnp.float32) * d ** (-0.5)
        w_out = jax.random.normal(ks[2], (d, d), dtype=jnp.float32) * d ** (-0.5)
        b_out = jnp.zeros((d,), dtype=jnp.float32)
        proj = jax.random.normal(ks[3], (HEADS, d // HEADS, f), dtype=jnp.float32) * (d // HEADS) ** (-0.5)
        return {'x': x, 'w_qkv': w_qkv, 'w_out': w_out, 'b_out': b_out, 'proj': proj}
    _L0_attn_in = _L0_attn_setup()

    def _L0_ffn_setup():
        import jax, jax.numpy as jnp
        import numpy as np
        HIDDEN = 128
        INTER = 512
        key = jax.random.key(seed)
        k1, k2, k3, k4, k5 = jax.random.split(key, 5)
        hidden_states = jax.random.normal(k1, (4, 256, HIDDEN), dtype=jnp.float32)
        W1 = jax.random.normal(k2, (HIDDEN, INTER), dtype=jnp.float32) * (1.0 / np.sqrt(HIDDEN))
        b1 = jax.random.normal(k3, (INTER,), dtype=jnp.float32) * 0.02
        W2 = jax.random.normal(k4, (INTER, HIDDEN), dtype=jnp.float32) * (1.0 / np.sqrt(INTER))
        b2 = jax.random.normal(k5, (HIDDEN,), dtype=jnp.float32) * 0.02
        return {'hidden_states': hidden_states, 'W1': W1, 'b1': b1, 'W2': W2, 'b2': b2}
    _L0_ffn_in = _L0_ffn_setup()
    _d = {'L0_attn_x': _L0_attn_in['x'], 'L0_attn_w_qkv': _L0_attn_in['w_qkv'], 'L0_attn_w_out': _L0_attn_in['w_out'], 'L0_attn_b_out': _L0_attn_in['b_out'], 'L0_attn_proj': _L0_attn_in['proj'], 'L0_ffn_W1': _L0_ffn_in['W1'], 'L0_ffn_b1': _L0_ffn_in['b1'], 'L0_ffn_W2': _L0_ffn_in['W2'], 'L0_ffn_b2': _L0_ffn_in['b2']}
    _x0 = _d['L0_attn_x']
    _d['L0_attn_x'] = jax.random.normal(jax.random.fold_in(jax.random.key(seed), 1), (4, 512, 128), dtype=_x0.dtype)
    del _x0
    return _d

def reference(L0_attn_x, L0_attn_w_qkv, L0_attn_w_out, L0_attn_b_out, L0_attn_proj, L0_ffn_W1, L0_ffn_b1, L0_ffn_W2, L0_ffn_b2):

    def _L0_attn_ref(x, w_qkv, w_out, b_out, proj):
        import jax, jax.numpy as jnp
        import numpy as np
        HEADS = 8
        BLOCK = 32
        b, n, d = x.shape
        h = HEADS
        hd = d // h
        nb = n // BLOCK
        qkv = x @ w_qkv.T
        q, k, v = jnp.split(qkv, 3, axis=-1)

        def to_blocks(t):
            return t.reshape(b, n, h, hd).transpose(0, 2, 1, 3).reshape(b, h, nb, BLOCK, hd)
        q, k, v = (to_blocks(q), to_blocks(k), to_blocks(v))
        qp = jax.nn.elu(jnp.einsum('bhcsd,hdf->bhcsf', q, proj)) + 1.0
        kp = jax.nn.elu(jnp.einsum('bhcsd,hdf->bhcsf', k, proj)) + 1.0
        kv = jnp.einsum('bhcsf,bhcsd->bhcfd', kp, v)
        num = jnp.einsum('bhcsf,bhcfd->bhcsd', qp, kv)
        ksum = kp.sum(axis=3)
        z = 1.0 / (jnp.einsum('bhcsf,bhcf->bhcs', qp, ksum) + 1e-08)
        out = num * z[..., None]
        out = out.reshape(b, h, n, hd).transpose(0, 2, 1, 3).reshape(b, n, d)
        return out @ w_out.T + b_out

    def _L0_ffn_ref(hidden_states, W1, b1, W2, b2):
        import jax, jax.numpy as jnp
        import numpy as np
        HIDDEN = 128
        INTER = 512
        h = jax.nn.relu(jnp.einsum('bsh,hi->bsi', hidden_states, W1) + b1)
        return jnp.einsum('bsi,ih->bsh', h, W2) + b2
    x = L0_attn_x
    x = x + 0.5 * _L0_ffn_ref(_layernorm(x, axis=-1), L0_ffn_W1, L0_ffn_b1, L0_ffn_W2, L0_ffn_b2)
    x = x + _L0_attn_ref(_layernorm(x, axis=-1), L0_attn_w_qkv, L0_attn_w_out, L0_attn_b_out, L0_attn_proj)
    x = x + 0.5 * _L0_ffn_ref(_layernorm(x, axis=-1), L0_ffn_W1, L0_ffn_b1, L0_ffn_W2, L0_ffn_b2)
    return x

_drawn_inputs = setup_inputs


def setup_inputs(seed=0):
    import zlib

    import numpy as np

    out = dict(_drawn_inputs(seed))
    spreads = {'L0_attn_b_out': (0.0, 0.1)}
    factors = {'L0_attn_proj': 4.806, 'L0_ffn_b1': 5.173, 'L0_ffn_b2': 3.11}
    for name, (base, spread) in spreads.items():
        noise = np.random.default_rng([zlib.crc32(name.encode()), seed]).standard_normal(out[name].shape)
        drawn = base * np.exp(spread * noise) if base else spread * noise
        out[name] = jnp.asarray(drawn.astype(out[name].dtype))
    for name, factor in factors.items():
        out[name] = (out[name] * factor).astype(out[name].dtype)
    return out
```

```python
from contextlib import ExitStack

import concourse.bass as bass
from concourse import mybir

F32 = mybir.dt.float32
F32R = mybir.dt.float32r
ALU = mybir.AluOpType
ACT = mybir.ActivationFunctionType

P = 128
D = 128
INTER = 512
NI = INTER // P
HEADS = 8
HD = D // HEADS
F = 128
BLOCK = 32
CHUNK = 512
NT = CHUNK // P
NB = P // BLOCK
VW = HD + 1
ROWS = 4 * HD
GROUP = 2
NG = HEADS // GROUP
FEAT_BUFS = 3
EPS = 1e-5
Z_EPS = 1e-8


def macaron_kernel(nc, x, w_qkv, w_out, b_out, proj, W1, b1, W2, b2, out):
    B, N, _ = x.shape
    NC = B * N // CHUNK
    x_chunks = x.rearrange("b n d -> (b n) d").rearrange("(c t p) d -> c p t d", p=P, t=NT)
    out_chunks = out.rearrange("b n d -> (b n) d").rearrange("(c t p) d -> c p t d", p=P, t=NT)

    with ExitStack() as ctx:
        def sb(name, shape, dt=F32):
            return ctx.enter_context(nc.sbuf_tensor(name, shape, dt))

        def sem(name):
            return ctx.enter_context(nc.semaphore(name))

        w1 = sb("w1", [P, INTER])
        w1_hi = sb("w1_hi", [P, INTER], F32R)
        w1_lo = sb("w1_lo", [P, INTER], F32R)
        w2 = sb("w2", [P, NI, D])
        wqkv_rows = sb("wqkv_rows", [P, 3, D])
        wqk_hi = sb("wqk_hi", [P, 2, D], F32R)
        wqk_lo = sb("wqk_lo", [P, 2, D], F32R)
        wv_hi = sb("wv_hi", [P, D], F32R)
        wv_lo = sb("wv_lo", [P, D], F32R)
        wout_rows = sb("wout_rows", [P, D])
        woutT = sb("woutT", [P, D])
        proj_rows = sb("proj_rows", [ROWS, HEADS, F])
        proj_round = sb("proj_round", [ROWS, HEADS, F], F32R)
        proj_packed = sb("proj_packed", [ROWS + 1, HEADS, F], F32R)
        bias_rows = sb("bias_rows", [NI + 1, D])
        bias_cols = sb("bias_cols", [P, NI + 1])
        bout_bc = sb("bout_bc", [P, D])
        ident = sb("ident", [P, P])
        minus_half = sb("minus_half", [P, NT])
        minus_one = sb("minus_one", [P, 1])

        x_in = sb("x_in", [P, NC, NT, D])
        x1 = sb("x1", [P, NT, D])
        x1_bout = sb("x1_bout", [P, NT, D])
        x2 = sb("x2", [P, NT, D])
        x2_kept = sb("x2_kept", [P, NT, D])
        x3 = sb("x3", [P, NT, D])
        stats = [sb(f"stats{k}", [P, NT, 6]) for k in range(3)]
        gap = [sb(f"gap{k}", [P, NT]) for k in range(3)]
        gap_sq = [sb(f"gap_sq{k}", [P, NT]) for k in range(3)]
        both = [sb(f"both{k}", [P, NT, 2]) for k in range(3)]
        spread = [sb(f"spread{k}", [P, NT]) for k in range(3)]
        mean = [sb(f"mean{k}", [P, NT]) for k in range(3)]
        var_eps = [sb(f"var_eps{k}", [P, NT]) for k in range(3)]
        rstd = [sb(f"rstd{k}", [P, NT]) for k in range(3)]
        xn = [sb(f"xn{k}", [P, NT, D]) for k in range(3)]
        xnT_hi = [sb(f"xnT_hi{k}", [P, CHUNK], F32R) for k in range(3)]
        xnT_lo = [sb(f"xnT_lo{k}", [P, CHUNK], F32R) for k in range(3)]
        hidden = [sb(f"hidden{k}", [P, NI, CHUNK]) for k in range(2)]
        yT = [sb(f"yT{k}", [P, CHUNK]) for k in range(2)]
        qk_hi = sb("qk_hi", [P, 2, CHUNK], F32R)
        qk_lo = sb("qk_lo", [P, 2, CHUNK], F32R)
        qk_packed = sb("qk_packed", [ROWS + 1, 2, HEADS, CHUNK], F32R)
        expo = sb("expo", [P, 2, 2, CHUNK])
        feat = sb("feat", [P, FEAT_BUFS, 2, CHUNK])
        scores_sb = sb("scores_sb", [P, 2, GROUP, NT, BLOCK])
        v_blocks = sb("v_blocks", [P, NT, HEADS, NB, VW])
        z = sb("z", [P, 2, HEADS // 2, NB])
        z_inv = sb("z_inv", [P, 2, HEADS // 2, NB])
        attn = sb("attn", [P, NB, HEADS, HD])
        attnT = sb("attnT", [P, NT, NB, BLOCK])

        wide = [ctx.enter_context(nc.psum_tensor(f"wide{i}", [P, 2, CHUNK], F32)) for i in range(2)]
        S = ctx.enter_context(nc.psum_tensor("S", [P, CHUNK], F32))[:, :]
        O = ctx.enter_context(nc.psum_tensor("O", [P, CHUNK], F32))[:, :]
        X = [ctx.enter_context(nc.psum_tensor(f"X{i}", [P, CHUNK], F32))[:, :] for i in range(2)]

        w_loaded = [sem(f"w_loaded{i}") for i in range(7)]
        x_first = sem("x_first")
        x_rest = sem("x_rest")
        qk_moved = sem("qk_moved")
        stored = sem("stored")
        pool_set = sem("pool_set")
        w_act = sem("w_act")
        consts = sem("consts")
        w_turned = sem("w_turned")
        w_split = sem("w_split")
        turned = [sem(f"turned{k}") for k in range(3)]
        hidden_sum = [sem(f"hidden_sum{k}") for k in range(2)]
        y_sum = [sem(f"y_sum{k}") for k in range(2)]
        y_turned = [sem(f"y_turned{k}") for k in range(2)]
        qk_sum = sem("qk_sum")
        v_sum = sem("v_sum")
        t_sum = sem("t_sum")
        scored = sem("scored")
        mixed = sem("mixed")
        attn_turned = sem("attn_turned")
        out_sum = sem("out_sum")
        exp_done = sem("exp_done")
        scores_out = sem("scores_out")
        xn_hi = [sem(f"xn_hi{k}") for k in range(3)]
        hidden_ready = [sem(f"hidden_ready{k}") for k in range(2)]
        y_ready = [sem(f"y_ready{k}") for k in range(2)]
        qk_hi_ready = sem("qk_hi_ready")
        v_ready = sem("v_ready")
        attnT_ready = sem("attnT_ready")
        stat_part = [sem(f"stat_part{k}") for k in range(3)]
        xn_ready = [sem(f"xn_ready{k}") for k in range(3)]
        xn_lo = [sem(f"xn_lo{k}") for k in range(3)]
        feat_ready = sem("feat_ready")
        z_part = sem("z_part")
        attn_ready = sem("attn_ready")
        x1_ready = sem("x1_ready")
        x2_ready = sem("x2_ready")
        x3_ready = sem("x3_ready")
        qk_lo_ready = sem("qk_lo_ready")
        rstd_ready = [sem(f"rstd_ready{k}") for k in range(3)]
        x1_bout_ready = sem("x1_bout_ready")
        x2_kept_ready = sem("x2_kept_ready")

        W_W1, W_QKV, W_BIAS, W_W2, W_PROJ, W_OUT, W_BOUT = range(7)

        def wait(eng, semaphore, count):
            if not isinstance(count, int) or count > 0:
                eng.wait_ge(semaphore, count)

        block = ctx.enter_context(nc.Block())

        def schedule(eng, step):
            step(0, ffn_a=False, prepare=True, ffn_b=False)
            with eng.Fori(1, NC - 1) as c:
                step(c, ffn_a=True, prepare=True, ffn_b=True)
            step(NC - 1, ffn_a=False, prepare=False, ffn_b=True)

        @block.sync
        def _(sp):
            def move_qk(c):
                wait(sp, qk_hi_ready, c + 1)
                for s in range(2):
                    for r in (0, 2 * HD):
                        sp.dma_start(qk_packed[r:r + HD, s, :, :].bitcast(F32),
                                     qk_hi[:, s, :].bitcast(F32)).then_inc(qk_moved, 16)
                wait(sp, qk_lo_ready, c + 1)
                for s in range(2):
                    for r in (HD, 3 * HD):
                        sp.dma_start(qk_packed[r:r + HD, s, :, :].bitcast(F32),
                                     qk_lo[:, s, :].bitcast(F32)).then_inc(qk_moved, 16)

            def store(c):
                wait(sp, x3_ready, c + 1)
                sp.dma_start(out_chunks[c], x3[:, :, :]).then_inc(stored, 16)

            def step(c, ffn_a, prepare, ffn_b):
                if prepare:
                    move_qk(c + 1)
                if ffn_b:
                    store(c - 1)

            sp.dma_start(x_in[:, 0, :, :], x_chunks[0]).then_inc(x_first, 16)
            sp.dma_start(w1[:, :], W1).then_inc(w_loaded[W_W1], 16)
            sp.dma_start(wqkv_rows[:, :, :], w_qkv.rearrange("(s r) d -> r s d", s=3)).then_inc(w_loaded[W_QKV], 16)
            sp.dma_start(w2[:, :, :], W2.rearrange("(i p) d -> p i d", p=P)).then_inc(w_loaded[W_W2], 16)
            for c in range(1, NC):
                sp.dma_start(x_in[:, c, :, :], x_chunks[c]).then_inc(x_rest, 16)
            move_qk(0)
            schedule(sp, step)
            store(NC - 1)
            sp.wait_ge(stored, 16 * NC)

        @block.tensor
        def _(pe):
            def turn_normed(k, c, bank):
                for t in range(NT):
                    wait(pe, xn_ready[k], NT * c + t + 1)
                    mm = pe.transpose(bank[:, t * P:(t + 1) * P], xn[k][:, t, :], ident[:, :])
                mm.then_inc(turned[k], 1)

            def split_product(bank, w_hi, w_lo, k, tokens=slice(0, CHUNK)):
                pe.matmul(bank, w_hi, xnT_hi[k][:, tokens], start=True, stop=False)
                pe.matmul(bank, w_lo, xnT_hi[k][:, tokens], start=False, stop=False)
                return pe.matmul(bank, w_hi, xnT_lo[k][:, tokens], start=False, stop=True)

            def ffn_up(k, i, bank):
                cols = slice(i * P, (i + 1) * P)
                split_product(bank, w1_hi[:, cols], w1_lo[:, cols], 2 * k).then_inc(hidden_sum[k], 1)

            def ffn_down(k, c, i, bank):
                wait(pe, hidden_ready[k], NI * c + i + 1)
                mm = pe.matmul(bank, w2[:, i, :], hidden[k][:, i, :], start=(i == 0), stop=(i == NI - 1))
                if i == NI - 1:
                    mm.then_inc(y_sum[k], 1)

            def turn_y(k, c, bank):
                wait(pe, y_ready[k], c + 1)
                for t in range(NT):
                    mm = pe.transpose(bank[:, t * P:(t + 1) * P], yT[k][:, t * P:(t + 1) * P], ident[:, :])
                mm.then_inc(y_turned[k], 1)

            def qk_product(c):
                wait(pe, xn_hi[1], c + 1)
                wait(pe, xn_lo[1], c + 1)
                for s in range(2):
                    mm = split_product(wide[0][:, s, :], wqk_hi[:, s, :], wqk_lo[:, s, :], 1)
                mm.then_inc(qk_sum, 1)

            def v_product(c):
                for t in range(NT):
                    bank, tokens = wide[1][:, 0, t * D:(t + 1) * D], slice(t * P, (t + 1) * P)
                    pe.matmul(bank, xnT_hi[1][:, tokens], wv_hi[:, :], start=True, stop=False)
                    pe.matmul(bank, xnT_hi[1][:, tokens], wv_lo[:, :], start=False, stop=False)
                    mm = pe.matmul(bank, xnT_lo[1][:, tokens], wv_hi[:, :], start=False, stop=True)
                mm.then_inc(v_sum, 1)

            def feature_product(c, h):
                for s in range(2):
                    mm = pe.matmul(wide[h % 2][:, s, :], proj_packed[:, h, :], qk_packed[:, s, h, :],
                                   start=True, stop=True)
                mm.then_inc(t_sum, 1)

            def score(c, h):
                g = h // GROUP
                wait(pe, feat_ready, HEADS * c + h + 1)
                if h and h % GROUP == 0:
                    wait(pe, scores_out, NG * c + h // GROUP)
                for t in range(NT):
                    for j in range(NB):
                        tok = slice(t * P + j * BLOCK, t * P + (j + 1) * BLOCK)
                        col = ((h % GROUP) * NT + t) * BLOCK
                        mm = pe.matmul(S[j * BLOCK:(j + 1) * BLOCK, col:col + BLOCK],
                                       feat[:, h % FEAT_BUFS, 1, tok], feat[:, h % FEAT_BUFS, 0, tok],
                                       start=True, stop=True)
                mm.then_inc(scored, 1)

            def mix(c, g):
                wait(pe, scores_out, NG * c + g + 1)
                for hh in range(GROUP):
                    h = g * GROUP + hh
                    col = (h % (HEADS // 2)) * NB * VW
                    for t in range(NT):
                        mm = pe.matmul(O[t * BLOCK:(t + 1) * BLOCK, col:col + NB * VW],
                                       scores_sb[:, g % 2, hh, t, :],
                                       v_blocks[:, t, h, :, :].rearrange("p j w -> p (j w)"),
                                       start=True, stop=True)
                mm.then_inc(mixed, 1)

            def turn_attn(c, bank):
                wait(pe, attn_ready, 2 * c + 2)
                for j in range(NB):
                    mm = pe.transpose(bank[:, j * P:(j + 1) * P],
                                      attn[:, j, :, :].rearrange("p h d -> p (h d)"), ident[:, :])
                mm.then_inc(attn_turned, 1)

            def out_product(c, bank):
                wait(pe, attnT_ready, c + 1)
                for t in range(NT):
                    mm = pe.matmul(bank[:, t * D:(t + 1) * D],
                                   attnT[:, t, :, :].rearrange("p j q -> p (j q)"), woutT[:, :],
                                   start=True, stop=True)
                mm.then_inc(out_sum, 1)

            def ffn_a_early(c):
                wait(pe, xn_lo[0], c + 1)
                for i in range(NI):
                    if i >= 2:
                        wait(pe, hidden_ready[0], NI * c + i - 1)
                    ffn_up(0, i, X[i % 2])
                wait(pe, hidden_ready[0], NI * c + 3)
                for i in range(NI):
                    ffn_down(0, c, i, X[0])
                turn_y(0, c, X[1])

            def step(c, ffn_a, prepare, ffn_b):
                wait(pe, qk_moved, 8 * 16 * (c + 1))
                feature_product(c, 0)
                if ffn_b:
                    turn_normed(2, c - 1, X[0])
                wait(pe, v_ready, NB * (c + 1))
                feature_product(c, 1)
                if ffn_a:
                    turn_normed(0, c + 1, X[1])
                wait(pe, feat_ready, HEADS * c + 1)
                feature_product(c, 2)
                score(c, 0)
                if ffn_a:
                    wait(pe, xn_lo[2], c)
                    wait(pe, xn_lo[0], c + 2)
                    ffn_up(0, 0, X[0])
                    ffn_up(0, 1, X[1])
                wait(pe, feat_ready, HEADS * c + 2)
                feature_product(c, 3)
                score(c, 1)
                if ffn_a:
                    wait(pe, hidden_ready[0], NI * (c + 1) + 1)
                    ffn_up(0, 2, X[0])
                    wait(pe, hidden_ready[0], NI * (c + 1) + 2)
                    ffn_up(0, 3, X[1])
                wait(pe, feat_ready, HEADS * c + 3)
                feature_product(c, 4)
                score(c, 2)
                wait(pe, x2_ready, c)
                mix(c, 0)
                if ffn_a:
                    wait(pe, hidden_ready[0], NI * (c + 1) + 3)
                    ffn_down(0, c + 1, 0, X[0])
                    ffn_down(0, c + 1, 1, X[0])
                wait(pe, feat_ready, HEADS * c + 4)
                feature_product(c, 5)
                score(c, 3)
                if ffn_a:
                    ffn_down(0, c + 1, 2, X[0])
                    ffn_down(0, c + 1, 3, X[0])
                wait(pe, feat_ready, HEADS * c + 5)
                feature_product(c, 6)
                score(c, 4)
                mix(c, 1)
                if ffn_a:
                    turn_y(0, c + 1, X[1])
                if ffn_b:
                    wait(pe, xn_lo[2], c)
                    ffn_up(1, 0, X[0])
                wait(pe, feat_ready, HEADS * c + 6)
                feature_product(c, 7)
                score(c, 5)
                if ffn_b:
                    if ffn_a:
                        wait(pe, x1_ready, c + 2)
                    ffn_up(1, 1, X[1])
                score(c, 6)
                wait(pe, attn_ready, 2 * c + 1)
                mix(c, 2)
                score(c, 7)
                if ffn_b:
                    wait(pe, hidden_ready[1], NI * (c - 1) + 1)
                    ffn_up(1, 2, X[0])
                    wait(pe, hidden_ready[1], NI * (c - 1) + 2)
                    ffn_up(1, 3, X[1])
                mix(c, 3)
                if prepare:
                    if ffn_b:
                        wait(pe, hidden_ready[1], NI * (c - 1) + 3)
                    turn_normed(1, c + 1, X[0])
                    wait(pe, feat_ready, HEADS * c + 7)
                    qk_product(c + 1)
                if ffn_b:
                    wait(pe, hidden_ready[1], NI * c)
                turn_attn(c, X[1])
                if prepare:
                    wait(pe, feat_ready, HEADS * c + 8)
                    v_product(c + 1)
                out_product(c, O)
                if ffn_b:
                    for i in range(NI):
                        ffn_down(1, c - 1, i, X[0])
                    turn_y(1, c - 1, X[1])

            pe.wait_ge(consts, 1)
            pe.wait_ge(w_loaded[W_BIAS], 32)
            pe.transpose(S[:, 0:NI + 1], bias_rows[:, :], ident[0:NI + 1, 0:NI + 1]).then_inc(w_turned, 1)
            turn_normed(0, 0, X[1])
            pe.wait_ge(w_loaded[W_QKV], 16)
            for s in range(3):
                pe.transpose(wide[1][:, 0, s * D:(s + 1) * D], wqkv_rows[:, s, :], ident[:, :])
            pe.wait_ge(w_loaded[W_OUT], 16)
            pe.transpose(wide[1][:, 0, 3 * D:4 * D], wout_rows[:, :], ident[:, :]).then_inc(w_turned, 1)
            pe.wait_ge(w_split, 2)
            pe.wait_ge(w_loaded[W_W2], 16)
            ffn_a_early(0)
            turn_normed(1, 0, X[0])
            pe.wait_ge(w_split, 9)
            qk_product(0)
            v_product(0)
            pe.wait_ge(x1_ready, 1)
            turn_normed(0, 1, X[1])
            ffn_a_early(1)
            pe.wait_ge(w_split, 12)
            pe.wait_ge(consts, 7)
            schedule(pe, step)
            turn_normed(2, NC - 1, X[0])
            pe.wait_ge(xn_lo[2], NC)
            ffn_up(1, 0, wide[0][:, 0, :])
            ffn_up(1, 1, wide[0][:, 1, :])
            ffn_up(1, 2, wide[1][:, 0, :])
            ffn_up(1, 3, wide[1][:, 1, :])
            for i in range(NI):
                ffn_down(1, NC - 1, i, X[0])
            turn_y(1, NC - 1, O)

        @block.scalar
        def _(act):
            def normed_hi(k, c, bank):
                wait(act, turned[k], c + 1)
                nc.scalar.copy(xnT_hi[k][:, :], bank).then_inc(xn_hi[k], 1)

            def relu(k, c, i, bank):
                wait(act, hidden_sum[k], NI * c + i + 1)
                nc.scalar.activation(hidden[k][:, i, :], bank, ACT.Relu,
                                     bias=bias_cols[:, i:i + 1]).then_inc(hidden_ready[k], 1)

            def y_out(k, c, bank):
                wait(act, y_sum[k], c + 1)
                nc.scalar.activation(yT[k][:, :], bank, ACT.Identity, bias=bias_cols[:, NI:NI + 1],
                                     scale=0.5).then_inc(y_ready[k], 1)

            def exp(c, h):
                wait(act, t_sum, HEADS * c + h + 1)
                wait(act, feat_ready, HEADS * c + h - 1)
                nc.scalar.activation(expo[:, h % 2, :, :], wide[h % 2][:, :, :], ACT.Exp,
                                     bias=minus_one[:, 0:1]).then_inc(exp_done, 1)

            def scores_copy(c, g):
                wait(act, scored, HEADS * c + GROUP * (g + 1))
                wait(act, mixed, NG * c + g - 1)
                nc.scalar.copy(scores_sb[:, g % 2, :, :, :].rearrange("p h t q -> p (h t q)"),
                               S[:, 0:GROUP * NT * BLOCK]).then_inc(scores_out, 1)

            def qk_copy(c):
                wait(act, qk_sum, c + 1)
                wait(act, qk_moved, 8 * 16 * c)
                nc.scalar.copy(qk_hi[:, :, :], wide[0][:, :, :]).then_inc(qk_hi_ready, 1)

            def v_copy(c):
                wait(act, v_sum, c + 1)
                wait(act, mixed, NG * c)
                for j in range(NB):
                    rows = slice(j * BLOCK, (j + 1) * BLOCK)
                    nc.scalar.copy(v_blocks[rows, :, :, j, 0:HD].rearrange("p t h d -> p (t h) d"),
                                   wide[1][rows, 0, :].rearrange("p (th d) -> p th d", d=HD)).then_inc(v_ready, 1)

            def attn_copy(c):
                wait(act, attn_turned, c + 1)
                wait(act, out_sum, c)
                nc.scalar.copy(attnT[:, :, :, :].rearrange("p t j q -> p j t q"),
                               X[1].rearrange("p (j t q) -> p j t q", j=NB, t=NT)).then_inc(attnT_ready, 1)

            def step(c, ffn_a, prepare, ffn_b):
                exp(c, 0)
                if ffn_b:
                    normed_hi(2, c - 1, X[0])
                exp(c, 1)
                if ffn_a:
                    normed_hi(0, c + 1, X[1])
                exp(c, 2)
                if ffn_a:
                    relu(0, c + 1, 0, X[0])
                    relu(0, c + 1, 1, X[1])
                scores_copy(c, 0)
                exp(c, 3)
                if ffn_a:
                    relu(0, c + 1, 2, X[0])
                    relu(0, c + 1, 3, X[1])
                exp(c, 4)
                scores_copy(c, 1)
                exp(c, 5)
                if ffn_a:
                    y_out(0, c + 1, X[0])
                exp(c, 6)
                scores_copy(c, 2)
                if ffn_b:
                    relu(1, c - 1, 0, X[0])
                exp(c, 7)
                if ffn_b:
                    relu(1, c - 1, 1, X[1])
                scores_copy(c, 3)
                if ffn_b:
                    relu(1, c - 1, 2, X[0])
                    relu(1, c - 1, 3, X[1])
                if prepare:
                    normed_hi(1, c + 1, X[0])
                    qk_copy(c + 1)
                attn_copy(c)
                if prepare:
                    v_copy(c + 1)
                if ffn_b:
                    y_out(1, c - 1, X[0])

            act.dma_start(bias_rows[0:NI, :], b1.rearrange("(i p) -> i p", p=P)).then_inc(w_loaded[W_BIAS], 16)
            act.dma_start(bias_rows[NI:NI + 1, :], b2.rearrange("(a d) -> a d", a=1)).then_inc(w_loaded[W_BIAS], 16)
            act.dma_start(wout_rows[:, :], w_out).then_inc(w_loaded[W_OUT], 16)
            for r in range(0, ROWS, HD):
                act.dma_start(proj_rows[r:r + HD, :, :], proj.rearrange("h d f -> d h f")).then_inc(w_loaded[W_PROJ], 16)
            act.dma_start(bout_bc[:, :], b_out.rearrange("(a d) -> a d", a=1).broadcast_to([P, D])).then_inc(w_loaded[W_BOUT], 16)
            act.wait_ge(w_turned, 1)
            nc.scalar.copy(bias_cols[:, 0:NI], S[:, 0:NI])
            nc.scalar.mul(bias_cols[:, NI:NI + 1], S[:, NI:NI + 1], 0.5).then_inc(w_act, 1)
            normed_hi(0, 0, X[1])
            act.wait_ge(w_act, 1)
            for i in range(NI):
                relu(0, 0, i, X[i % 2])
            y_out(0, 0, X[0])
            normed_hi(1, 0, X[0])
            qk_copy(0)
            act.wait_ge(consts, 7)
            v_copy(0)
            normed_hi(0, 1, X[1])
            for i in range(NI):
                relu(0, 1, i, X[i % 2])
            y_out(0, 1, X[0])
            schedule(act, step)
            normed_hi(2, NC - 1, X[0])
            for i in range(NI):
                relu(1, NC - 1, i, wide[i // 2][:, i % 2, :])
            y_out(1, NC - 1, X[0])

        @block.vector
        def _(dve):
            def norm_stats(k, c, src):
                base = 4 * c
                for t in range(NT):
                    bn = nc.vector.bn_stats(stats[k][:, t, :], src[:, t, :])
                bn.then_inc(stat_part[k], 1)
                even, odd = stats[k][:, :, 0:3], stats[k][:, :, 3:6]
                wait(dve, stat_part[k], base + 1)
                nc.vector.tensor_tensor(gap[k][:, :], even[:, :, 1], odd[:, :, 1], ALU.subtract)
                nc.vector.tensor_tensor(both[k][:, :, :], even[:, :, 1:3], odd[:, :, 1:3], ALU.add).then_inc(stat_part[k], 1)
                wait(dve, stat_part[k], base + 2)
                nc.vector.tensor_tensor(gap_sq[k][:, :], gap[k][:, :], gap[k][:, :], ALU.mult)
                nc.vector.tensor_scalar(mean[k][:, :], both[k][:, :, 0], 0.5, None, ALU.mult)
                nc.vector.tensor_scalar(spread[k][:, :], both[k][:, :, 1], 1.0 / D, EPS, ALU.mult, ALU.add).then_inc(stat_part[k], 1)
                wait(dve, stat_part[k], base + 3)
                nc.vector.scalar_tensor_tensor(out=var_eps[k][:, :], in0=gap_sq[k][:, :], scalar=0.25,
                                               in1=spread[k][:, :], op0=ALU.mult, op1=ALU.add).then_inc(stat_part[k], 1)

            def norm_apply(k, c, src):
                wait(dve, rstd_ready[k], c + 1)
                for t in range(NT):
                    nc.vector.tensor_scalar(xn[k][:, t, :], src[:, t, :], mean[k][:, t:t + 1],
                                            rstd[k][:, t:t + 1], ALU.subtract, ALU.mult).then_inc(xn_ready[k], 1)

            def normed_lo(k, c, bank):
                wait(dve, xn_hi[k], c + 1)
                nc.vector.tensor_tensor(xnT_lo[k][:, :], bank, xnT_hi[k][:, :].bitcast(F32),
                                        ALU.subtract).then_inc(xn_lo[k], 1)

            def feature(c, h):
                wait(dve, exp_done, HEADS * c + h + 1)
                wait(dve, scored, HEADS * c + h + 1 - FEAT_BUFS if h >= FEAT_BUFS else HEADS * c)
                nc.vector.scalar_tensor_tensor(
                    out=feat[:, h % FEAT_BUFS, :, :], in0=expo[:, h % 2, :, :], scalar=1.0,
                    in1=wide[h % 2][:, :, :], op0=ALU.min, op1=ALU.max).then_inc(feat_ready, 1)

            def divide(c, half):
                n = HEADS // 2
                sums = O[:, 0:n * NB * VW].rearrange("p (h j w) -> p h j w", h=n, j=NB)
                wait(dve, mixed, NG * c + 2 * (half + 1))
                nc.vector.tensor_scalar(z[:, half, :, :], sums[:, :, :, HD], Z_EPS, None,
                                        ALU.add).then_inc(z_part, 1)
                wait(dve, z_part, 4 * c + 2 * half + 1)
                nc.vector.reciprocal(z_inv[:, half, :, :], z[:, half, :, :]).then_inc(z_part, 1)
                wait(dve, z_part, 4 * c + 2 * half + 2)
                wait(dve, attn_turned, c)
                nc.vector.tensor_tensor(
                    attn[:, :, n * half:n * (half + 1), :].rearrange("p j h d -> p h j d"),
                    sums[:, :, :, 0:HD],
                    z_inv[:, half, :, :].rearrange("p h (j a) -> p h j a", a=1).broadcast_to([P, n, NB, HD]),
                    ALU.mult).then_inc(attn_ready, 1)

            def step(c, ffn_a, prepare, ffn_b):
                if ffn_b:
                    norm_apply(2, c - 1, x2)
                if ffn_a:
                    norm_stats(0, c + 1, x_in[:, c + 1, :, :])
                feature(c, 0)
                if ffn_b:
                    normed_lo(2, c - 1, X[0])
                if ffn_a:
                    norm_apply(0, c + 1, x_in[:, c + 1, :, :])
                feature(c, 1)
                if ffn_a:
                    normed_lo(0, c + 1, X[1])
                for h in range(2, 6):
                    feature(c, h)
                divide(c, 0)
                feature(c, 6)
                if ffn_a:
                    ffn_a_residual(c + 1)
                    norm_stats(1, c + 1, x1)
                feature(c, 7)
                if prepare:
                    norm_apply(1, c + 1, x1)
                divide(c, 1)
                if prepare:
                    normed_lo(1, c + 1, X[0])
                    qk_lo_part(c + 1)
                wait(dve, out_sum, c + 1)
                wait(dve, x1_bout_ready, c + 1)
                if ffn_b:
                    wait(dve, x2_kept_ready, c)
                add_residual(x2, x1_bout, O, x2_ready)
                wait(dve, x2_ready, c + 1)
                norm_stats(2, c, x2)
                if ffn_b:
                    wait(dve, y_turned[1], c)
                    if not prepare:
                        wait(dve, stored, 16 * (c - 1))
                    add_residual(x3, x2_kept, X[1], x3_ready)

            def ffn_a_residual(c):
                wait(dve, y_turned[0], c + 1)
                wait(dve, x1_bout_ready, c)
                add_residual(x1, x_in[:, c, :, :], X[1], x1_ready)
                wait(dve, x1_ready, c + 1)

            def add_residual(dst, src, bank, ready):
                nc.vector.tensor_tensor(dst[:, :, :], src[:, :, :], bank.rearrange("p (t d) -> p t d", d=D),
                                        ALU.add).then_inc(ready, 1)

            def qk_lo_part(c):
                wait(dve, qk_hi_ready, c + 1)
                wait(dve, qk_moved, 8 * 16 * c)
                nc.vector.tensor_tensor(qk_lo[:, :, :], wide[0][:, :, :], qk_hi[:, :, :].bitcast(F32),
                                        ALU.subtract).then_inc(qk_lo_ready, 1)

            dve.wait_ge(x_first, 16)
            norm_stats(0, 0, x_in[:, 0, :, :])
            dve.wait_ge(w_loaded[W_W1], 16)
            nc.vector.tensor_copy(w1_hi[:, :], w1[:, :]).then_inc(w_split, 1)
            dve.wait_ge(w_split, 1)
            nc.vector.tensor_tensor(w1_lo[:, :], w1[:, :], w1_hi[:, :].bitcast(F32), ALU.subtract).then_inc(w_split, 1)
            norm_apply(0, 0, x_in[:, 0, :, :])
            normed_lo(0, 0, X[1])
            dve.wait_ge(w_turned, 2)
            turned_w = wide[1][:, 0, :].rearrange("p (s c) -> p s c", c=D)
            for s in range(2):
                nc.vector.tensor_copy(wqk_hi[:, s, :].rearrange("p (d h) -> p d h", h=HEADS),
                                      turned_w[:, s, :].rearrange("p (h d) -> p d h", h=HEADS)).then_inc(w_split, 1)
            nc.vector.tensor_copy(wv_hi[:, :], turned_w[:, 2, :]).then_inc(w_split, 1)
            dve.wait_ge(w_split, 5)
            for s in range(2):
                nc.vector.tensor_tensor(wqk_lo[:, s, :].rearrange("p (d h) -> p d h", h=HEADS),
                                        turned_w[:, s, :].rearrange("p (h d) -> p d h", h=HEADS),
                                        wqk_hi[:, s, :].rearrange("p (d h) -> p d h", h=HEADS).bitcast(F32),
                                        ALU.subtract).then_inc(w_split, 1)
            nc.vector.tensor_tensor(wv_lo[:, :], turned_w[:, 2, :], wv_hi[:, :].bitcast(F32),
                                    ALU.subtract).then_inc(w_split, 1)
            nc.vector.tensor_copy(woutT[:, :], turned_w[:, 3, :]).then_inc(w_split, 1)
            dve.wait_ge(w_loaded[W_PROJ], 16 * 4)
            nc.vector.tensor_copy(proj_round[:, :, :], proj_rows[:, :, :]).then_inc(w_split, 1)
            nc.vector.tensor_copy(proj_packed[0:2 * HD, :, :], proj_rows[0:2 * HD, :, :]).then_inc(w_split, 1)
            dve.wait_ge(w_split, 10)
            nc.vector.tensor_tensor(proj_packed[2 * HD:ROWS, :, :], proj_rows[2 * HD:ROWS, :, :],
                                    proj_round[2 * HD:ROWS, :, :].bitcast(F32), ALU.subtract).then_inc(w_split, 1)
            dve.wait_ge(x_rest, 16 * (NC - 1))
            norm_stats(0, 1, x_in[:, 1, :, :])
            ffn_a_residual(0)
            norm_stats(1, 0, x1)
            norm_apply(0, 1, x_in[:, 1, :, :])
            norm_apply(1, 0, x1)
            normed_lo(1, 0, X[0])
            qk_lo_part(0)
            normed_lo(0, 1, X[1])
            ffn_a_residual(1)
            norm_stats(1, 1, x1)
            schedule(dve, step)
            norm_apply(2, NC - 1, x2)
            normed_lo(2, NC - 1, X[0])
            dve.wait_ge(y_turned[1], NC)
            dve.wait_ge(x2_kept_ready, NC)
            dve.wait_ge(stored, 16 * (NC - 1))
            add_residual(x3, x2_kept, O, x3_ready)

        @block.gpsimd
        def _(pool):
            def reciprocal_root(k, c):
                wait(pool, stat_part[k], 4 * (c + 1))
                nc.gpsimd.tensor_tensor(rstd[k][:, :], var_eps[k][:, :], minus_half[:, :], ALU.pow).then_inc(rstd_ready[k], 1)

            def add_bout(c):
                wait(pool, x1_ready, c + 1)
                wait(pool, x2_ready, c)
                nc.gpsimd.tensor_tensor(x1_bout[:, :, :], x1[:, :, :],
                                        bout_bc[:, :].rearrange("p (a d) -> p a d", a=1).broadcast_to([P, NT, D]),
                                        ALU.add).then_inc(x1_bout_ready, 1)

            def keep_x2(c):
                nc.gpsimd.tensor_copy(x2_kept[:, :, :], x2[:, :, :]).then_inc(x2_kept_ready, 1)

            def step(c, ffn_a, prepare, ffn_b):
                if ffn_a:
                    reciprocal_root(0, c + 1)
                if ffn_b:
                    keep_x2(c - 1)
                if ffn_a:
                    reciprocal_root(1, c + 1)
                reciprocal_root(2, c)
                if prepare:
                    add_bout(c + 1)
                if ffn_b:
                    wait(pool, stored, 16 * c)

            nc.gpsimd.memset(minus_half[:, :], -0.5).then_inc(pool_set, 1)
            nc.gpsimd.memset(ident[:, :], 0.0).then_inc(pool_set, 1)
            pool.wait_ge(pool_set, 2)
            nc.gpsimd.affine_select(out=ident[:, :], in_=ident[:, :], compare_op=ALU.not_equal, fill=1.0,
                                    base=0, pattern=[[-1, P]], channel_multiplier=1).then_inc(consts, 1)
            reciprocal_root(0, 0)
            nc.gpsimd.memset(minus_one[:, :], -1.0).then_inc(pool_set, 1)
            pool.wait_ge(pool_set, 3)
            nc.gpsimd.memset(proj_packed[ROWS:ROWS + 1, :, :].bitcast(F32), 1.0)
            nc.gpsimd.memset(qk_packed[ROWS:ROWS + 1, :, :, :].bitcast(F32), 1.0).then_inc(consts, 1)
            pool.wait_ge(consts, 2)
            nc.gpsimd.memset(v_blocks[:, :, :, :, :], 0.0).then_inc(consts, 1)
            pool.wait_ge(consts, 3)
            for j in range(NB):
                nc.gpsimd.memset(v_blocks[j * BLOCK:(j + 1) * BLOCK, :, :, j, HD:VW], 1.0).then_inc(consts, 1)
                pool.wait_ge(consts, 4 + j)
            pool.wait_ge(w_loaded[W_BOUT], 16)
            reciprocal_root(0, 1)
            reciprocal_root(1, 0)
            add_bout(0)
            reciprocal_root(1, 1)
            schedule(pool, step)
            keep_x2(NC - 1)


_INS = ['L0_attn_x', 'L0_attn_w_qkv', 'L0_attn_w_out', 'L0_attn_b_out', 'L0_attn_proj',
        'L0_ffn_W1', 'L0_ffn_b1', 'L0_ffn_W2', 'L0_ffn_b2']


def kernel(**inputs):
    import numpy as _np
    import concourse.bacc as _bacc
    from concourse import mybir as _mybir
    from concourse.bass_utils import run_bass_kernel_spmd as _run

    nc = _bacc.Bacc("TRN2", target_bir_lowering=False, num_devices=1)
    arrays, args = {}, []
    for name in _INS:
        a = _np.ascontiguousarray(inputs[name])
        arrays[f"in_{name}_dram"] = a
        args.append(nc.dram_tensor(f"in_{name}_dram", a.shape, _mybir.dt.from_np(a.dtype), kind="ExternalInput").ap())
    shape = inputs['L0_attn_x'].shape
    args.append(nc.dram_tensor("out_0_dram", shape, _mybir.dt.from_np(_np.dtype("float32")), kind="ExternalOutput").ap())
    macaron_kernel(nc, *args)
    r = _run(nc, [arrays], core_ids=[0])
    return r.results[0]["out_0_dram"]
```

```python
from contextlib import ExitStack

import concourse.bass as bass
from concourse import mybir

F32 = mybir.dt.float32
F32R = mybir.dt.float32r
ALU = mybir.AluOpType
ACT = mybir.ActivationFunctionType

P = 128
D = 128
INTER = 512
NI = INTER // P
HEADS = 8
HD = D // HEADS
F = 128
BLOCK = 32
CHUNK = 512
NT = CHUNK // P
NB = P // BLOCK
VW = HD + 1
ROWS = 4 * HD
HALF = HEADS // 2
GROUP = 2
NG = HEADS // GROUP
FEAT_BUFS = 3
EPS = 1e-5
Z_EPS = 1e-8


def macaron_kernel(nc, x, w_qkv, w_out, b_out, proj, W1, b1, W2, b2, out):
    B, N, _ = x.shape
    NC = B * N // CHUNK
    x_chunks = x.rearrange("b n d -> (b n) d").rearrange("(c t p) d -> c p t d", p=P, t=NT)
    out_chunks = out.rearrange("b n d -> (b n) d").rearrange("(c t p) d -> c p t d", p=P, t=NT)

    with ExitStack() as ctx:
        def sb(name, shape, dt=F32):
            return ctx.enter_context(nc.sbuf_tensor(name, shape, dt))

        def sem(name):
            return ctx.enter_context(nc.semaphore(name))

        w1 = sb("w1", [P, INTER])
        w1_hi = sb("w1_hi", [P, INTER], F32R)
        w1_lo = sb("w1_lo", [P, INTER], F32R)
        w2 = sb("w2", [P, NI, D])
        wqkv_rows = sb("wqkv_rows", [P, 3, D])
        wqk_hi = sb("wqk_hi", [P, 2, D], F32R)
        wqk_lo = sb("wqk_lo", [P, 2, D], F32R)
        wv_hi = sb("wv_hi", [P, D], F32R)
        wv_lo = sb("wv_lo", [P, D], F32R)
        wout_rows = sb("wout_rows", [P, D])
        woutT = sb("woutT", [P, D])
        proj_rows = sb("proj_rows", [ROWS, HEADS, F])
        proj_round = sb("proj_round", [ROWS, HEADS, F], F32R)
        proj_packed = sb("proj_packed", [ROWS + 1, HEADS, F], F32R)
        bias_rows = sb("bias_rows", [NI + 1, D])
        bias_cols = sb("bias_cols", [P, NI + 1])
        bout_bc = sb("bout_bc", [P, D])
        ident = sb("ident", [P, P])
        minus_half = sb("minus_half", [P, NC * NT])
        minus_one = sb("minus_one", [P, 1])

        x_in = sb("x_in", [P, NC, NT, D])
        x1 = sb("x1", [P, NT, D])
        x1_bout = sb("x1_bout", [P, NT, D])
        x2 = sb("x2", [P, NT, D])
        x2_kept = sb("x2_kept", [P, NT, D])
        x3 = sb("x3", [P, NT, D])
        tiles = [NC * NT, NT, NT]
        stats = [sb(f"stats{k}", [P, tiles[k], 6]) for k in range(3)]
        gap = [sb(f"gap{k}", [P, tiles[k]]) for k in range(3)]
        gap_sq = [sb(f"gap_sq{k}", [P, tiles[k]]) for k in range(3)]
        both = [sb(f"both{k}", [P, tiles[k], 2]) for k in range(3)]
        spread = [sb(f"spread{k}", [P, tiles[k]]) for k in range(3)]
        mean = [sb(f"mean{k}", [P, tiles[k]]) for k in range(3)]
        var_eps = [sb(f"var_eps{k}", [P, tiles[k]]) for k in range(3)]
        rstd = [sb(f"rstd{k}", [P, tiles[k]]) for k in range(3)]
        xn = [sb(f"xn{k}", [P, tiles[k], D]) for k in range(3)]
        xnT_hi = [sb(f"xnT_hi{k}", [P, tiles[k] * P], F32R) for k in range(3)]
        xnT_lo = [sb(f"xnT_lo{k}", [P, tiles[k] * P], F32R) for k in range(3)]
        hidden = [sb(f"hidden{k}", [P, NI, CHUNK]) for k in range(2)]
        yT = [sb(f"yT{k}", [P, CHUNK]) for k in range(2)]
        qk_hi = sb("qk_hi", [P, 2, CHUNK], F32R)
        qk_lo = sb("qk_lo", [P, 2, CHUNK], F32R)
        qk_packed = sb("qk_packed", [ROWS + 1, HEADS, 2, CHUNK], F32R)
        expo = sb("expo", [P, 2, 2, CHUNK])
        feat = sb("feat", [P, FEAT_BUFS, 2, CHUNK])
        scores_sb = sb("scores_sb", [P, 2, GROUP, NT, BLOCK])
        v_blocks = sb("v_blocks", [P, NT, HEADS, NB, VW])
        z = sb("z", [P, 2, HALF, NB])
        z_inv = sb("z_inv", [P, 2, HALF, NB])
        attn = sb("attn", [P, NB, HEADS, HD])
        attnT = sb("attnT", [P, NT, NB, BLOCK])

        wide = [ctx.enter_context(nc.psum_tensor(f"wide{i}", [P, 2, CHUNK], F32)) for i in range(2)]
        S = ctx.enter_context(nc.psum_tensor("S", [P, CHUNK], F32))[:, :]
        O = ctx.enter_context(nc.psum_tensor("O", [P, CHUNK], F32))[:, :]
        X = [ctx.enter_context(nc.psum_tensor(f"X{i}", [P, CHUNK], F32))[:, :] for i in range(2)]

        w_loaded = [sem(f"w_loaded{i}") for i in range(7)]
        x_first = sem("x_first")
        x_rest = sem("x_rest")
        qk_moved = [sem(f"qk_moved{g}") for g in range(2)]
        stored = sem("stored")
        pool_set = sem("pool_set")
        w_act = sem("w_act")
        consts = sem("consts")
        w_turned = sem("w_turned")
        w_split = sem("w_split")
        turned = [sem(f"turned{k}") for k in range(3)]
        hidden_sum = [sem(f"hidden_sum{k}") for k in range(2)]
        y_sum = [sem(f"y_sum{k}") for k in range(2)]
        y_turned = [sem(f"y_turned{k}") for k in range(2)]
        qk_sum = sem("qk_sum")
        v_sum = sem("v_sum")
        t_sum = sem("t_sum")
        scored = sem("scored")
        mixed = sem("mixed")
        attn_turned = sem("attn_turned")
        out_sum = sem("out_sum")
        exp_done = sem("exp_done")
        scores_out = sem("scores_out")
        xn_hi = [sem(f"xn_hi{k}") for k in range(3)]
        hidden_ready = [sem(f"hidden_ready{k}") for k in range(2)]
        y_ready = [sem(f"y_ready{k}") for k in range(2)]
        q_hi_ready = sem("q_hi_ready")
        v_ready = sem("v_ready")
        attnT_ready = sem("attnT_ready")
        stat_part = [sem(f"stat_part{k}") for k in range(3)]
        xn_ready = [sem(f"xn_ready{k}") for k in range(3)]
        xn_lo = [sem(f"xn_lo{k}") for k in range(3)]
        feat_ready = sem("feat_ready")
        z_part = sem("z_part")
        attn_ready = sem("attn_ready")
        x1_ready = sem("x1_ready")
        x2_ready = sem("x2_ready")
        x3_ready = sem("x3_ready")
        k_hi_ready = sem("k_hi_ready")
        qk_lo_ready = sem("qk_lo_ready")
        rstd_ready = [sem(f"rstd_ready{k}") for k in range(3)]
        x1_bout_ready = sem("x1_bout_ready")
        x2_kept_ready = sem("x2_kept_ready")

        W_W1, W_QKV, W_BIAS, W_W2, W_PROJ, W_OUT, W_BOUT = range(7)

        def wait(eng, semaphore, count):
            if not isinstance(count, int) or count > 0:
                eng.wait_ge(semaphore, count)

        block = ctx.enter_context(nc.Block())

        def schedule(eng, step):
            step(0, ahead=True, ffn_b=False)
            with eng.Fori(1, NC - 1) as c:
                step(c, ahead=True, ffn_b=True)
            step(NC - 1, ahead=False, ffn_b=True)

        @block.sync
        def _(sp):
            def move_qk(c):
                def spread_rows(source, g, first):
                    heads = slice(g * HALF, (g + 1) * HALF)
                    for r in (first, first + 2 * HD):
                        sp.dma_start(qk_packed[r:r + HD, heads, :, :].bitcast(F32),
                                     source[g * HALF * HD:(g + 1) * HALF * HD, :, :].bitcast(F32)
                                     ).then_inc(qk_moved[g], 16)

                wait(sp, q_hi_ready, c + 1)
                wait(sp, k_hi_ready, c + 1)
                spread_rows(qk_hi, 0, 0)
                wait(sp, qk_lo_ready, 2 * c + 2)
                spread_rows(qk_lo, 0, HD)
                spread_rows(qk_hi, 1, 0)
                spread_rows(qk_lo, 1, HD)

            def store(c):
                wait(sp, x3_ready, c + 1)
                sp.dma_start(out_chunks[c], x3[:, :, :]).then_inc(stored, 16)

            def step(c, ahead, ffn_b):
                if ahead:
                    move_qk(c + 1)
                if ffn_b:
                    store(c - 1)

            sp.dma_start(x_in[:, 0, :, :], x_chunks[0]).then_inc(x_first, 16)
            sp.dma_start(w1[:, :], W1).then_inc(w_loaded[W_W1], 16)
            sp.dma_start(wqkv_rows[:, :, :], w_qkv.rearrange("(s r) d -> r s d", s=3)).then_inc(w_loaded[W_QKV], 16)
            sp.dma_start(w2[:, :, :], W2.rearrange("(i p) d -> p i d", p=P)).then_inc(w_loaded[W_W2], 16)
            for c in range(1, NC):
                sp.dma_start(x_in[:, c, :, :], x_chunks[c]).then_inc(x_rest, 16)
            move_qk(0)
            schedule(sp, step)
            store(NC - 1)
            sp.wait_ge(stored, 16 * NC)

        @block.tensor
        def _(pe):
            def turn_normed(k, c, bank):
                first = NT * c if k == 0 else 0
                for t in range(NT):
                    wait(pe, xn_ready[k], NT * c + t + 1)
                    mm = pe.transpose(bank[:, t * P:(t + 1) * P], xn[k][:, first + t, :], ident[:, :])
                mm.then_inc(turned[k], 1)

            def split_product(bank, w_hi, w_lo, k, tokens=slice(0, CHUNK)):
                pe.matmul(bank, w_hi, xnT_hi[k][:, tokens], start=True, stop=False)
                pe.matmul(bank, w_lo, xnT_hi[k][:, tokens], start=False, stop=False)
                return pe.matmul(bank, w_hi, xnT_lo[k][:, tokens], start=False, stop=True)

            def ffn_up(k, c, i, bank):
                cols = slice(i * P, (i + 1) * P)
                tokens = bass.ds(c * CHUNK, CHUNK) if k == 0 else slice(0, CHUNK)
                split_product(bank, w1_hi[:, cols], w1_lo[:, cols], 2 * k, tokens).then_inc(hidden_sum[k], 1)

            def ffn_down(k, c, i, bank):
                wait(pe, hidden_ready[k], NI * c + i + 1)
                mm = pe.matmul(bank, w2[:, i, :], hidden[k][:, i, :], start=(i == 0), stop=(i == NI - 1))
                if i == NI - 1:
                    mm.then_inc(y_sum[k], 1)

            def turn_y(k, c, bank):
                wait(pe, y_ready[k], c + 1)
                for t in range(NT):
                    mm = pe.transpose(bank[:, t * P:(t + 1) * P], yT[k][:, t * P:(t + 1) * P], ident[:, :])
                mm.then_inc(y_turned[k], 1)

            def qk_product(c):
                wait(pe, xn_hi[1], c + 1)
                wait(pe, xn_lo[1], c + 1)
                for s in range(2):
                    split_product(wide[0][:, s, :], wqk_hi[:, s, :], wqk_lo[:, s, :], 1).then_inc(qk_sum, 1)

            def v_product(c):
                for t in range(NT):
                    bank, tokens = wide[1][:, 0, t * D:(t + 1) * D], slice(t * P, (t + 1) * P)
                    pe.matmul(bank, xnT_hi[1][:, tokens], wv_hi[:, :], start=True, stop=False)
                    pe.matmul(bank, xnT_hi[1][:, tokens], wv_lo[:, :], start=False, stop=False)
                    mm = pe.matmul(bank, xnT_lo[1][:, tokens], wv_hi[:, :], start=False, stop=True)
                mm.then_inc(v_sum, 1)

            def feature_product(c, h):
                for s in range(2):
                    mm = pe.matmul(wide[h % 2][:, s, :], proj_packed[:, h, :], qk_packed[:, h, s, :],
                                   start=True, stop=True)
                mm.then_inc(t_sum, 1)

            def first_features(c):
                wait(pe, qk_moved[0], 4 * 16 * (c + 1))
                feature_product(c, 0)
                wait(pe, v_ready, NB * (c + 1))
                feature_product(c, 1)

            def score(c, h):
                g = h // GROUP
                wait(pe, feat_ready, HEADS * c + h + 1)
                if h and h % GROUP == 0:
                    wait(pe, scores_out, NG * c + h // GROUP)
                for t in range(NT):
                    for j in range(NB):
                        tok = slice(t * P + j * BLOCK, t * P + (j + 1) * BLOCK)
                        col = ((h % GROUP) * NT + t) * BLOCK
                        mm = pe.matmul(S[j * BLOCK:(j + 1) * BLOCK, col:col + BLOCK],
                                       feat[:, h % FEAT_BUFS, 1, tok], feat[:, h % FEAT_BUFS, 0, tok],
                                       start=True, stop=True)
                mm.then_inc(scored, 1)

            def mix(c, g):
                wait(pe, scores_out, NG * c + g + 1)
                for hh in range(GROUP):
                    h = g * GROUP + hh
                    col = (h % (HALF)) * NB * VW
                    for t in range(NT):
                        mm = pe.matmul(O[t * BLOCK:(t + 1) * BLOCK, col:col + NB * VW],
                                       scores_sb[:, g % 2, hh, t, :],
                                       v_blocks[:, t, h, :, :].rearrange("p j w -> p (j w)"),
                                       start=True, stop=True)
                mm.then_inc(mixed, 1)

            def turn_attn(c, bank):
                wait(pe, attn_ready, 2 * c + 2)
                for j in range(NB):
                    mm = pe.transpose(bank[:, j * P:(j + 1) * P],
                                      attn[:, j, :, :].rearrange("p h d -> p (h d)"), ident[:, :])
                mm.then_inc(attn_turned, 1)

            def out_product(c, bank):
                wait(pe, attnT_ready, c + 1)
                for t in range(NT):
                    mm = pe.matmul(bank[:, t * D:(t + 1) * D],
                                   attnT[:, t, :, :].rearrange("p j q -> p (j q)"), woutT[:, :],
                                   start=True, stop=True)
                mm.then_inc(out_sum, 1)

            def step(c, ahead, ffn_b):
                if ffn_b:
                    turn_normed(2, c - 1, O)
                if ahead:
                    wait(pe, xn_lo[0], NC)
                    ffn_up(0, c + 1, 0, X[0])
                    ffn_up(0, c + 1, 1, X[1])
                    wait(pe, hidden_ready[0], NI * (c + 1) + 1)
                    ffn_up(0, c + 1, 2, X[0])
                wait(pe, feat_ready, HEADS * c + 1)
                feature_product(c, 2)
                if ahead:
                    wait(pe, hidden_ready[0], NI * (c + 1) + 2)
                    ffn_up(0, c + 1, 3, X[1])
                wait(pe, feat_ready, HEADS * c + 2)
                feature_product(c, 3)
                score(c, 0)
                score(c, 1)
                if ahead:
                    wait(pe, hidden_ready[0], NI * (c + 1) + 3)
                    ffn_down(0, c + 1, 0, X[0])
                    ffn_down(0, c + 1, 1, X[0])
                wait(pe, feat_ready, HEADS * c + 3)
                wait(pe, qk_moved[1], 4 * 16 * (c + 1))
                feature_product(c, 4)
                score(c, 2)
                if ahead:
                    ffn_down(0, c + 1, 2, X[0])
                    ffn_down(0, c + 1, 3, X[0])
                wait(pe, feat_ready, HEADS * c + 4)
                feature_product(c, 5)
                score(c, 3)
                if ahead:
                    turn_y(0, c + 1, X[1])
                if ffn_b:
                    wait(pe, xn_lo[2], c)
                mix(c, 0)
                wait(pe, feat_ready, HEADS * c + 5)
                feature_product(c, 6)
                score(c, 4)
                mix(c, 1)
                if ffn_b:
                    ffn_up(1, c - 1, 0, X[0])
                wait(pe, feat_ready, HEADS * c + 6)
                feature_product(c, 7)
                score(c, 5)
                if ffn_b:
                    if ahead:
                        wait(pe, x1_ready, c + 2)
                    ffn_up(1, c - 1, 1, X[1])
                score(c, 6)
                if ffn_b:
                    wait(pe, hidden_ready[1], NI * (c - 1) + 2)
                if ahead:
                    if not ffn_b:
                        wait(pe, x1_ready, c + 2)
                    turn_normed(1, c + 1, X[1])
                if ffn_b:
                    ffn_up(1, c - 1, 2, X[0])
                score(c, 7)
                if ahead:
                    wait(pe, feat_ready, HEADS * c + 7)
                    qk_product(c + 1)
                wait(pe, attn_ready, 2 * c + 1)
                mix(c, 2)
                if ffn_b:
                    wait(pe, hidden_ready[1], NI * (c - 1) + 3)
                    ffn_up(1, c - 1, 3, X[0])
                if ahead:
                    wait(pe, feat_ready, HEADS * c + 8)
                    v_product(c + 1)
                mix(c, 3)
                if ffn_b:
                    wait(pe, hidden_ready[1], NI * c)
                    ffn_down(1, c - 1, 0, X[0])
                turn_attn(c, X[1])
                if ffn_b:
                    ffn_down(1, c - 1, 1, X[0])
                out_product(c, O)
                if ahead:
                    first_features(c + 1)
                if ffn_b:
                    ffn_down(1, c - 1, 2, X[0])
                    ffn_down(1, c - 1, 3, X[0])
                    turn_y(1, c - 1, S)

            pe.wait_ge(consts, 1)
            pe.wait_ge(w_loaded[W_BIAS], 32)
            pe.transpose(S[:, 0:NI + 1], bias_rows[:, :], ident[0:NI + 1, 0:NI + 1]).then_inc(w_turned, 1)
            turn_normed(0, 0, X[1])
            pe.wait_ge(w_loaded[W_QKV], 16)
            for s in range(3):
                pe.transpose(wide[1][:, 0, s * D:(s + 1) * D], wqkv_rows[:, s, :], ident[:, :])
            pe.wait_ge(w_loaded[W_OUT], 16)
            pe.transpose(wide[1][:, 0, 3 * D:4 * D], wout_rows[:, :], ident[:, :]).then_inc(w_turned, 1)
            pe.wait_ge(w_split, 2)
            pe.wait_ge(w_loaded[W_W2], 16)
            wait(pe, xn_lo[0], 1)
            for i in range(NI):
                if i >= 2:
                    wait(pe, hidden_ready[0], i - 1)
                ffn_up(0, 0, i, X[i % 2])
            for c in range(1, NC):
                turn_normed(0, c, wide[0][:, c % 2, :] if c < 3 else O)
            wait(pe, hidden_ready[0], 3)
            for i in range(NI):
                ffn_down(0, 0, i, X[0])
            turn_y(0, 0, X[1])
            wait(pe, x1_ready, 1)
            turn_normed(1, 0, X[1])
            pe.wait_ge(w_split, 9)
            pe.wait_ge(xn_lo[0], NC)
            qk_product(0)
            v_product(0)
            pe.wait_ge(w_split, 12)
            pe.wait_ge(consts, 7)
            first_features(0)
            schedule(pe, step)
            turn_normed(2, NC - 1, O)
            pe.wait_ge(xn_lo[2], NC)
            ffn_up(1, NC - 1, 0, wide[0][:, 0, :])
            ffn_up(1, NC - 1, 1, wide[0][:, 1, :])
            ffn_up(1, NC - 1, 2, wide[1][:, 0, :])
            ffn_up(1, NC - 1, 3, wide[1][:, 1, :])
            for i in range(NI):
                ffn_down(1, NC - 1, i, X[0])
            turn_y(1, NC - 1, X[1])

        @block.scalar
        def _(act):
            def normed_hi(k, c, bank):
                wait(act, turned[k], c + 1)
                tokens = slice(c * CHUNK, (c + 1) * CHUNK) if k == 0 else slice(0, CHUNK)
                nc.scalar.copy(xnT_hi[k][:, tokens], bank).then_inc(xn_hi[k], 1)

            def relu(k, c, i, bank):
                wait(act, hidden_sum[k], NI * c + i + 1)
                nc.scalar.activation(hidden[k][:, i, :], bank, ACT.Relu,
                                     bias=bias_cols[:, i:i + 1]).then_inc(hidden_ready[k], 1)

            def y_out(k, c, bank):
                wait(act, y_sum[k], c + 1)
                nc.scalar.activation(yT[k][:, :], bank, ACT.Identity, bias=bias_cols[:, NI:NI + 1],
                                     scale=0.5).then_inc(y_ready[k], 1)

            def exp(c, h):
                wait(act, t_sum, HEADS * c + h + 1)
                wait(act, feat_ready, HEADS * c + h - 1)
                nc.scalar.activation(expo[:, h % 2, :, :], wide[h % 2][:, :, :], ACT.Exp,
                                     bias=minus_one[:, 0:1]).then_inc(exp_done, 1)

            def scores_copy(c, g):
                wait(act, scored, HEADS * c + GROUP * (g + 1))
                wait(act, mixed, NG * c + g - 1)
                nc.scalar.copy(scores_sb[:, g % 2, :, :, :].rearrange("p h t q -> p (h t q)"),
                               S[:, 0:GROUP * NT * BLOCK]).then_inc(scores_out, 1)

            def q_hi_copy(c):
                wait(act, qk_sum, 2 * c + 1)
                for g in range(2):
                    wait(act, qk_moved[g], 4 * 16 * c)
                nc.scalar.copy(qk_hi[:, 0, :], wide[0][:, 0, :]).then_inc(q_hi_ready, 1)

            def v_copy(c):
                wait(act, v_sum, c + 1)
                wait(act, mixed, NG * c)
                for j in range(NB):
                    rows = slice(j * BLOCK, (j + 1) * BLOCK)
                    nc.scalar.copy(v_blocks[rows, :, :, j, 0:HD].rearrange("p t h d -> p (t h) d"),
                                   wide[1][rows, 0, :].rearrange("p (th d) -> p th d", d=HD)).then_inc(v_ready, 1)

            def attn_copy(c):
                wait(act, attn_turned, c + 1)
                wait(act, out_sum, c)
                nc.scalar.copy(attnT[:, :, :, :].rearrange("p t j q -> p j t q"),
                               X[1].rearrange("p (j t q) -> p j t q", j=NB, t=NT)).then_inc(attnT_ready, 1)

            def step(c, ahead, ffn_b):
                if ffn_b:
                    normed_hi(2, c - 1, O)
                if ahead:
                    relu(0, c + 1, 0, X[0])
                    relu(0, c + 1, 1, X[1])
                exp(c, 2)
                if ahead:
                    relu(0, c + 1, 2, X[0])
                exp(c, 3)
                if ahead:
                    relu(0, c + 1, 3, X[1])
                scores_copy(c, 0)
                exp(c, 4)
                if ahead:
                    y_out(0, c + 1, X[0])
                exp(c, 5)
                scores_copy(c, 1)
                exp(c, 6)
                if ffn_b:
                    relu(1, c - 1, 0, X[0])
                exp(c, 7)
                scores_copy(c, 2)
                if ffn_b:
                    relu(1, c - 1, 1, X[1])
                if ahead:
                    normed_hi(1, c + 1, X[1])
                if ffn_b:
                    relu(1, c - 1, 2, X[0])
                scores_copy(c, 3)
                if ahead:
                    q_hi_copy(c + 1)
                if ffn_b:
                    relu(1, c - 1, 3, X[0])
                if ahead:
                    v_copy(c + 1)
                attn_copy(c)
                if ahead:
                    exp(c + 1, 0)
                    exp(c + 1, 1)
                if ffn_b:
                    y_out(1, c - 1, X[0])

            act.dma_start(bias_rows[0:NI, :], b1.rearrange("(i p) -> i p", p=P)).then_inc(w_loaded[W_BIAS], 16)
            act.dma_start(bias_rows[NI:NI + 1, :], b2.rearrange("(a d) -> a d", a=1)).then_inc(w_loaded[W_BIAS], 16)
            act.dma_start(wout_rows[:, :], w_out).then_inc(w_loaded[W_OUT], 16)
            for r in range(0, ROWS, HD):
                act.dma_start(proj_rows[r:r + HD, :, :], proj.rearrange("h d f -> d h f")).then_inc(w_loaded[W_PROJ], 16)
            act.dma_start(bout_bc[:, :], b_out.rearrange("(a d) -> a d", a=1).broadcast_to([P, D])).then_inc(w_loaded[W_BOUT], 16)
            act.wait_ge(w_turned, 1)
            nc.scalar.copy(bias_cols[:, 0:NI], S[:, 0:NI])
            nc.scalar.mul(bias_cols[:, NI:NI + 1], S[:, NI:NI + 1], 0.5).then_inc(w_act, 1)
            normed_hi(0, 0, X[1])
            act.wait_ge(w_act, 1)
            for i in range(NI):
                relu(0, 0, i, X[i % 2])
            for c in range(1, NC):
                normed_hi(0, c, wide[0][:, c % 2, :] if c < 3 else O)
            y_out(0, 0, X[0])
            normed_hi(1, 0, X[1])
            q_hi_copy(0)
            act.wait_ge(consts, 7)
            v_copy(0)
            exp(0, 0)
            exp(0, 1)
            schedule(act, step)
            normed_hi(2, NC - 1, O)
            for i in range(NI):
                relu(1, NC - 1, i, wide[i // 2][:, i % 2, :])
            y_out(1, NC - 1, X[0])

        @block.vector
        def _(dve):
            def norm_stats(k, n, src, tiles=slice(0, NT)):
                base = 4 * n
                for t in range(tiles.stop - tiles.start):
                    bn = nc.vector.bn_stats(stats[k][:, tiles.start + t, :], src[:, t, :])
                bn.then_inc(stat_part[k], 1)
                even, odd = stats[k][:, tiles, 0:3], stats[k][:, tiles, 3:6]
                wait(dve, stat_part[k], base + 1)
                nc.vector.tensor_tensor(gap[k][:, tiles], even[:, :, 1], odd[:, :, 1], ALU.subtract)
                nc.vector.tensor_tensor(both[k][:, tiles, :], even[:, :, 1:3], odd[:, :, 1:3], ALU.add).then_inc(stat_part[k], 1)
                wait(dve, stat_part[k], base + 2)
                nc.vector.tensor_tensor(gap_sq[k][:, tiles], gap[k][:, tiles], gap[k][:, tiles], ALU.mult)
                nc.vector.tensor_scalar(mean[k][:, tiles], both[k][:, tiles, 0], 0.5, None, ALU.mult)
                nc.vector.tensor_scalar(spread[k][:, tiles], both[k][:, tiles, 1], 1.0 / D, EPS, ALU.mult, ALU.add).then_inc(stat_part[k], 1)
                wait(dve, stat_part[k], base + 3)
                nc.vector.scalar_tensor_tensor(out=var_eps[k][:, tiles], in0=gap_sq[k][:, tiles], scalar=0.25,
                                               in1=spread[k][:, tiles], op0=ALU.mult, op1=ALU.add).then_inc(stat_part[k], 1)

            def norm_apply(k, n, src, tiles=slice(0, NT)):
                wait(dve, rstd_ready[k], n + 1)
                for t in range(tiles.start, tiles.stop):
                    nc.vector.tensor_scalar(xn[k][:, t, :], src[:, t - tiles.start, :], mean[k][:, t:t + 1],
                                            rstd[k][:, t:t + 1], ALU.subtract, ALU.mult).then_inc(xn_ready[k], 1)

            def normed_lo(k, c, bank):
                tokens = slice(c * CHUNK, (c + 1) * CHUNK) if k == 0 else slice(0, CHUNK)
                wait(dve, xn_hi[k], c + 1)
                nc.vector.tensor_tensor(xnT_lo[k][:, tokens], bank, xnT_hi[k][:, tokens].bitcast(F32),
                                        ALU.subtract).then_inc(xn_lo[k], 1)

            def feature(c, h):
                wait(dve, exp_done, HEADS * c + h + 1)
                wait(dve, scored, HEADS * c + h + 1 - FEAT_BUFS if h >= FEAT_BUFS else HEADS * c)
                nc.vector.scalar_tensor_tensor(
                    out=feat[:, h % FEAT_BUFS, :, :], in0=expo[:, h % 2, :, :], scalar=1.0,
                    in1=wide[h % 2][:, :, :], op0=ALU.min, op1=ALU.max).then_inc(feat_ready, 1)

            def divide(c, half):
                n = HALF
                sums = O[:, 0:n * NB * VW].rearrange("p (h j w) -> p h j w", h=n, j=NB)
                wait(dve, mixed, NG * c + 2 * (half + 1))
                nc.vector.tensor_scalar(z[:, half, :, :], sums[:, :, :, HD], Z_EPS, None,
                                        ALU.add).then_inc(z_part, 1)
                wait(dve, z_part, 4 * c + 2 * half + 1)
                nc.vector.reciprocal(z_inv[:, half, :, :], z[:, half, :, :]).then_inc(z_part, 1)
                wait(dve, z_part, 4 * c + 2 * half + 2)
                wait(dve, attn_turned, c)
                nc.vector.tensor_tensor(
                    attn[:, :, n * half:n * (half + 1), :].rearrange("p j h d -> p h j d"),
                    sums[:, :, :, 0:HD],
                    z_inv[:, half, :, :].rearrange("p h (j a) -> p h j a", a=1).broadcast_to([P, n, NB, HD]),
                    ALU.mult).then_inc(attn_ready, 1)

            def step(c, ahead, ffn_b):
                feature(c, 1)
                if ffn_b:
                    normed_lo(2, c - 1, O)
                for h in range(2, 5):
                    feature(c, h)
                if ahead:
                    ffn_a_residual(c + 1)
                feature(c, 5)
                if ahead:
                    norm_stats(1, c + 1, x1)
                feature(c, 6)
                if ahead:
                    norm_apply(1, c + 1, x1)
                feature(c, 7)
                if ahead:
                    normed_lo(1, c + 1, X[1])
                divide(c, 0)
                if ahead:
                    qk_parts(c + 1)
                divide(c, 1)
                wait(dve, out_sum, c + 1)
                wait(dve, x1_bout_ready, c + 1)
                if ffn_b:
                    wait(dve, x2_kept_ready, c)
                add_residual(x2, x1_bout, O, x2_ready)
                wait(dve, x2_ready, c + 1)
                norm_stats(2, c, x2)
                if ahead:
                    feature(c + 1, 0)
                norm_apply(2, c, x2)
                if ffn_b:
                    wait(dve, y_turned[1], c)
                    if not ahead:
                        wait(dve, stored, 16 * (c - 1))
                    add_residual(x3, x2_kept, S, x3_ready)

            def ffn_a_residual(c):
                wait(dve, y_turned[0], c + 1)
                wait(dve, x1_bout_ready, c)
                add_residual(x1, x_in[:, c, :, :], X[1], x1_ready)
                wait(dve, x1_ready, c + 1)

            def add_residual(dst, src, bank, ready):
                nc.vector.tensor_tensor(dst[:, :, :], src[:, :, :], bank.rearrange("p (t d) -> p t d", d=D),
                                        ALU.add).then_inc(ready, 1)

            def qk_parts(c):
                wait(dve, qk_sum, 2 * c + 2)
                for g in range(2):
                    wait(dve, qk_moved[g], 4 * 16 * c)
                nc.vector.tensor_copy(qk_hi[:, 1, :], wide[0][:, 1, :]).then_inc(k_hi_ready, 1)
                for s, ready in ((0, q_hi_ready), (1, k_hi_ready)):
                    wait(dve, ready, c + 1)
                    nc.vector.tensor_tensor(qk_lo[:, s, :], wide[0][:, s, :], qk_hi[:, s, :].bitcast(F32),
                                            ALU.subtract).then_inc(qk_lo_ready, 1)

            dve.wait_ge(x_first, 16)
            norm_stats(0, 0, x_in[:, 0, :, :])
            dve.wait_ge(w_loaded[W_W1], 16)
            nc.vector.tensor_copy(w1_hi[:, :], w1[:, :]).then_inc(w_split, 1)
            dve.wait_ge(w_split, 1)
            nc.vector.tensor_tensor(w1_lo[:, :], w1[:, :], w1_hi[:, :].bitcast(F32), ALU.subtract).then_inc(w_split, 1)
            norm_apply(0, 0, x_in[:, 0, :, :])
            normed_lo(0, 0, X[1])
            dve.wait_ge(w_turned, 2)
            turned_w = wide[1][:, 0, :].rearrange("p (s c) -> p s c", c=D)
            for s in range(2):
                nc.vector.tensor_copy(wqk_hi[:, s, :].rearrange("p (g d h) -> p g d h", g=2, h=HALF),
                                      turned_w[:, s, :].rearrange("p (g h d) -> p g d h", g=2, h=HALF)).then_inc(w_split, 1)
            nc.vector.tensor_copy(wv_hi[:, :], turned_w[:, 2, :]).then_inc(w_split, 1)
            dve.wait_ge(w_split, 5)
            for s in range(2):
                nc.vector.tensor_tensor(wqk_lo[:, s, :].rearrange("p (g d h) -> p g d h", g=2, h=HALF),
                                        turned_w[:, s, :].rearrange("p (g h d) -> p g d h", g=2, h=HALF),
                                        wqk_hi[:, s, :].rearrange("p (g d h) -> p g d h", g=2, h=HALF).bitcast(F32),
                                        ALU.subtract).then_inc(w_split, 1)
            nc.vector.tensor_tensor(wv_lo[:, :], turned_w[:, 2, :], wv_hi[:, :].bitcast(F32),
                                    ALU.subtract).then_inc(w_split, 1)
            nc.vector.tensor_copy(woutT[:, :], turned_w[:, 3, :]).then_inc(w_split, 1)
            dve.wait_ge(w_loaded[W_PROJ], 16 * 4)
            nc.vector.tensor_copy(proj_round[:, :, :], proj_rows[:, :, :]).then_inc(w_split, 1)
            nc.vector.tensor_copy(proj_packed[0:2 * HD, :, :], proj_rows[0:2 * HD, :, :]).then_inc(w_split, 1)
            dve.wait_ge(w_split, 10)
            nc.vector.tensor_tensor(proj_packed[2 * HD:ROWS, :, :], proj_rows[2 * HD:ROWS, :, :],
                                    proj_round[2 * HD:ROWS, :, :].bitcast(F32), ALU.subtract).then_inc(w_split, 1)
            dve.wait_ge(x_rest, 16 * (NC - 1))
            others = slice(NT, NC * NT)
            norm_stats(0, 1, x_in[:, 1:, :, :].rearrange("p c t d -> p (c t) d"), others)
            norm_apply(0, 1, x_in[:, 1:, :, :].rearrange("p c t d -> p (c t) d"), others)
            for c in range(1, NC):
                normed_lo(0, c, wide[0][:, c % 2, :] if c < 3 else O)
            ffn_a_residual(0)
            norm_stats(1, 0, x1)
            norm_apply(1, 0, x1)
            normed_lo(1, 0, X[1])
            qk_parts(0)
            feature(0, 0)
            schedule(dve, step)
            normed_lo(2, NC - 1, O)
            dve.wait_ge(y_turned[1], NC)
            dve.wait_ge(x2_kept_ready, NC)
            dve.wait_ge(stored, 16 * (NC - 1))
            add_residual(x3, x2_kept, X[1], x3_ready)

        @block.gpsimd
        def _(pool):
            def reciprocal_root(k, n, tiles=slice(0, NT)):
                wait(pool, stat_part[k], 4 * (n + 1))
                nc.gpsimd.tensor_tensor(rstd[k][:, tiles], var_eps[k][:, tiles], minus_half[:, tiles], ALU.pow).then_inc(rstd_ready[k], 1)

            def add_bout(c):
                wait(pool, x1_ready, c + 1)
                wait(pool, x2_ready, c)
                nc.gpsimd.tensor_tensor(x1_bout[:, :, :], x1[:, :, :],
                                        bout_bc[:, :].rearrange("p (a d) -> p a d", a=1).broadcast_to([P, NT, D]),
                                        ALU.add).then_inc(x1_bout_ready, 1)

            def keep_x2(c):
                nc.gpsimd.tensor_copy(x2_kept[:, :, :], x2[:, :, :]).then_inc(x2_kept_ready, 1)

            def step(c, ahead, ffn_b):
                if ffn_b:
                    keep_x2(c - 1)
                if ahead:
                    reciprocal_root(1, c + 1)
                reciprocal_root(2, c)
                if ahead:
                    add_bout(c + 1)
                if ffn_b:
                    wait(pool, stored, 16 * c)

            nc.gpsimd.memset(minus_half[:, :], -0.5).then_inc(pool_set, 1)
            nc.gpsimd.memset(ident[:, :], 0.0).then_inc(pool_set, 1)
            pool.wait_ge(pool_set, 2)
            nc.gpsimd.affine_select(out=ident[:, :], in_=ident[:, :], compare_op=ALU.not_equal, fill=1.0,
                                    base=0, pattern=[[-1, P]], channel_multiplier=1).then_inc(consts, 1)
            reciprocal_root(0, 0)
            nc.gpsimd.memset(minus_one[:, :], -1.0).then_inc(pool_set, 1)
            pool.wait_ge(pool_set, 3)
            nc.gpsimd.memset(proj_packed[ROWS:ROWS + 1, :, :].bitcast(F32), 1.0)
            nc.gpsimd.memset(qk_packed[ROWS:ROWS + 1, :, :, :].bitcast(F32), 1.0).then_inc(consts, 1)
            pool.wait_ge(consts, 2)
            nc.gpsimd.memset(v_blocks[:, :, :, :, :], 0.0).then_inc(consts, 1)
            pool.wait_ge(consts, 3)
            for j in range(NB):
                nc.gpsimd.memset(v_blocks[j * BLOCK:(j + 1) * BLOCK, :, :, j, HD:VW], 1.0).then_inc(consts, 1)
                pool.wait_ge(consts, 4 + j)
            pool.wait_ge(w_loaded[W_BOUT], 16)
            reciprocal_root(0, 1, slice(NT, NC * NT))
            reciprocal_root(1, 0)
            add_bout(0)
            schedule(pool, step)
            keep_x2(NC - 1)


_INS = ['L0_attn_x', 'L0_attn_w_qkv', 'L0_attn_w_out', 'L0_attn_b_out', 'L0_attn_proj',
        'L0_ffn_W1', 'L0_ffn_b1', 'L0_ffn_W2', 'L0_ffn_b2']


def kernel(**inputs):
    import numpy as _np
    import concourse.bacc as _bacc
    from concourse import mybir as _mybir
    from concourse.bass_utils import run_bass_kernel_spmd as _run

    nc = _bacc.Bacc("TRN2", target_bir_lowering=False, num_devices=1)
    arrays, args = {}, []
    for name in _INS:
        a = _np.ascontiguousarray(inputs[name])
        arrays[f"in_{name}_dram"] = a
        args.append(nc.dram_tensor(f"in_{name}_dram", a.shape, _mybir.dt.from_np(a.dtype), kind="ExternalInput").ap())
    shape = inputs['L0_attn_x'].shape
    args.append(nc.dram_tensor("out_0_dram", shape, _mybir.dt.from_np(_np.dtype("float32")), kind="ExternalOutput").ap())
    macaron_kernel(nc, *args)
    r = _run(nc, [arrays], core_ids=[0])
    return r.results[0]["out_0_dram"]
```

```python
from contextlib import ExitStack

import concourse.bass as bass
from concourse import mybir

F32 = mybir.dt.float32
F32R = mybir.dt.float32r
ALU = mybir.AluOpType
ACT = mybir.ActivationFunctionType

P = 128
D = 128
INTER = 512
NI = INTER // P
HEADS = 8
HD = D // HEADS
F = 128
BLOCK = 32
CHUNK = 512
NT = CHUNK // P
NB = P // BLOCK
VW = HD + 1
ROWS = 4 * HD
HALF = HEADS // 2
GROUP = 2
NG = HEADS // GROUP
FEAT_BUFS = 3
EPS = 1e-5
Z_EPS = 1e-8


def macaron_kernel(nc, x, w_qkv, w_out, b_out, proj, W1, b1, W2, b2, out):
    B, N, _ = x.shape
    NC = B * N // CHUNK
    x_chunks = x.rearrange("b n d -> (b n) d").rearrange("(c t p) d -> c p t d", p=P, t=NT)
    x_others = x.rearrange("b n d -> (b n) d")[CHUNK:, :].rearrange("(t p) d -> p t d", p=P)
    out_chunks = out.rearrange("b n d -> (b n) d").rearrange("(c t p) d -> c p t d", p=P, t=NT)

    with ExitStack() as ctx:
        def sb(name, shape, dt=F32):
            return ctx.enter_context(nc.sbuf_tensor(name, shape, dt))

        def sem(name):
            return ctx.enter_context(nc.semaphore(name))

        w1 = sb("w1", [P, INTER])
        w1_hi = sb("w1_hi", [P, INTER], F32R)
        w1_lo = sb("w1_lo", [P, INTER], F32R)
        w2 = sb("w2", [P, NI, D])
        wqkv_rows = sb("wqkv_rows", [P, 3, D])
        wqk_hi = sb("wqk_hi", [P, 2, D], F32R)
        wqk_lo = sb("wqk_lo", [P, 2, D], F32R)
        wv_hi = sb("wv_hi", [P, D], F32R)
        wv_lo = sb("wv_lo", [P, D], F32R)
        wout_rows = sb("wout_rows", [P, D])
        woutT = sb("woutT", [P, D])
        proj_rows = sb("proj_rows", [ROWS, HEADS, F])
        proj_round = sb("proj_round", [ROWS, HEADS, F], F32R)
        proj_packed = sb("proj_packed", [ROWS + 1, HEADS, F], F32R)
        b1_rows = sb("b1_rows", [NI, P])
        b1_cols = sb("b1_cols", [P, NI])
        b2_bc = sb("b2_bc", [P, D])
        b2_half = sb("b2_half", [P, D])
        bout_bc = sb("bout_bc", [P, D])
        ident = sb("ident", [P, P])
        minus_half = sb("minus_half", [P, NC * NT])
        minus_one = sb("minus_one", [P, 1])
        ones = sb("ones", [P, HEADS * 2 * CHUNK // P])

        x_in = sb("x_in", [P, NC, NT, D])
        x_b2 = sb("x_b2", [P, NC, NT, D])
        x1 = sb("x1", [P, NT, D])
        x1_bout = sb("x1_bout", [P, NT, D])
        x2 = sb("x2", [P, NT, D])
        x2_b2 = sb("x2_b2", [P, NT, D])
        x3 = sb("x3", [P, NT, D])
        tiles = [NC * NT, NT, NT]
        stats = [sb(f"stats{k}", [P, tiles[k], 6]) for k in range(3)]
        gap = [sb(f"gap{k}", [P, tiles[k]]) for k in range(3)]
        gap_sq = [sb(f"gap_sq{k}", [P, tiles[k]]) for k in range(3)]
        both = [sb(f"both{k}", [P, tiles[k], 2]) for k in range(3)]
        spread = [sb(f"spread{k}", [P, tiles[k]]) for k in range(3)]
        mean = [sb(f"mean{k}", [P, tiles[k]]) for k in range(3)]
        var_eps = [sb(f"var_eps{k}", [P, tiles[k]]) for k in range(3)]
        rstd = [sb(f"rstd{k}", [P, tiles[k]]) for k in range(3)]
        xn = [sb(f"xn{k}", [P, tiles[k], D]) for k in range(3)]
        xnT_hi = [sb(f"xnT_hi{k}", [P, tiles[k] * P], F32R) for k in range(3)]
        xnT_lo = [sb(f"xnT_lo{k}", [P, tiles[k] * P], F32R) for k in range(3)]
        hidden = [sb(f"hidden{k}", [P, NI, CHUNK]) for k in range(2)]
        qk_hi = sb("qk_hi", [P, 2, CHUNK], F32R)
        qk_lo = sb("qk_lo", [P, 2, CHUNK], F32R)
        qk_packed = sb("qk_packed", [ROWS + 1, HEADS, 2, CHUNK], F32R)
        expo = sb("expo", [P, 2, 2, CHUNK])
        feat = sb("feat", [P, FEAT_BUFS, 2, CHUNK])
        scores_sb = sb("scores_sb", [P, 2, GROUP, NT, BLOCK])
        v_blocks = sb("v_blocks", [P, NT, HEADS, NB, VW])
        z = sb("z", [P, 2, HALF, NB])
        z_inv = sb("z_inv", [P, 2, HALF, NB])
        attn = sb("attn", [P, NB, HEADS, HD])
        attnT = sb("attnT", [P, NT, NB, BLOCK])

        wide = [ctx.enter_context(nc.psum_tensor(f"wide{i}", [P, 2, CHUNK], F32)) for i in range(2)]
        S = ctx.enter_context(nc.psum_tensor("S", [P, CHUNK], F32))[:, :]
        O = ctx.enter_context(nc.psum_tensor("O", [P, CHUNK], F32))[:, :]
        X = [ctx.enter_context(nc.psum_tensor(f"X{i}", [P, CHUNK], F32))[:, :] for i in range(2)]

        w_loaded = [sem(f"w_loaded{i}") for i in range(9)]
        x_first = sem("x_first")
        x_rest = sem("x_rest")
        qk_moved = [sem(f"qk_moved{g}") for g in range(2)]
        stored = sem("stored")
        pool_set = sem("pool_set")
        w1_hi_ready = sem("w1_hi_ready")
        w_act = sem("w_act")
        consts = sem("consts")
        w_turned = sem("w_turned")
        w_split = sem("w_split")
        turned = [sem(f"turned{k}") for k in range(3)]
        hidden_sum = [sem(f"hidden_sum{k}") for k in range(2)]
        y_sum = [sem(f"y_sum{k}") for k in range(2)]
        qk_sum = sem("qk_sum")
        v_sum = sem("v_sum")
        t_sum = sem("t_sum")
        scored = sem("scored")
        mixed = sem("mixed")
        attn_turned = sem("attn_turned")
        out_sum = sem("out_sum")
        exp_done = sem("exp_done")
        scores_out = sem("scores_out")
        xn_hi = [sem(f"xn_hi{k}") for k in range(3)]
        hidden_ready = [sem(f"hidden_ready{k}") for k in range(2)]
        q_hi_ready = sem("q_hi_ready")
        v_ready = sem("v_ready")
        attnT_ready = sem("attnT_ready")
        stat_part = [sem(f"stat_part{k}") for k in range(3)]
        xn_ready = [sem(f"xn_ready{k}") for k in range(3)]
        xn_lo = [sem(f"xn_lo{k}") for k in range(3)]
        feat_ready = sem("feat_ready")
        z_part = sem("z_part")
        attn_ready = sem("attn_ready")
        x1_ready = sem("x1_ready")
        x2_ready = sem("x2_ready")
        x3_ready = sem("x3_ready")
        k_hi_ready = sem("k_hi_ready")
        qk_lo_ready = sem("qk_lo_ready")
        rstd_ready = [sem(f"rstd_ready{k}") for k in range(3)]
        x_b2_ready = sem("x_b2_ready")
        x1_bout_ready = sem("x1_bout_ready")
        x2_b2_ready = sem("x2_b2_ready")

        W_W1, W_QKV, W_B1, W_W2, W_PROJ, W_OUT, W_BOUT, W_B2, W_ONES = range(9)

        def wait(eng, semaphore, count):
            if not isinstance(count, int) or count > 0:
                eng.wait_ge(semaphore, count)

        TILES = [slice(0, NT // 2), slice(NT // 2, NT)]
        TOKENS = [slice(0, CHUNK // 2), slice(CHUNK // 2, CHUNK)]
        LAST_BANKS = [X[1], S]
        LAST_SUM_BANKS = [wide[0][:, 0, :], wide[0][:, 1, :], wide[1][:, 0, :], wide[1][:, 1, :]]
        FIRST_NORM_BANKS = [None, X[0], O, S]
        FIRST_SUM_BANKS = [O, S, wide[0][:, 0, :], wide[0][:, 1, :]]

        block = ctx.enter_context(nc.Block())

        def schedule(eng, step):
            step(0, ahead=True, ffn_b=False)
            with eng.Fori(1, NC - 1) as c:
                step(c, ahead=True, ffn_b=True)
            step(NC - 1, ahead=False, ffn_b=True)

        @block.sync
        def _(sp):
            def move_qk(c):
                def spread_rows(source, g, first):
                    heads = slice(g * HALF, (g + 1) * HALF)
                    for r in (first, first + 2 * HD):
                        sp.dma_start(qk_packed[r:r + HD, heads, :, :].bitcast(F32),
                                     source[g * HALF * HD:(g + 1) * HALF * HD, :, :].bitcast(F32)
                                     ).then_inc(qk_moved[g], 16)

                wait(sp, q_hi_ready, c + 1)
                wait(sp, k_hi_ready, c + 1)
                spread_rows(qk_hi, 0, 0)
                wait(sp, qk_lo_ready, 2 * c + 2)
                spread_rows(qk_lo, 0, HD)
                spread_rows(qk_hi, 1, 0)
                spread_rows(qk_lo, 1, HD)

            def store(c):
                wait(sp, x3_ready, c + 1)
                sp.dma_start(out_chunks[c], x3[:, :, :]).then_inc(stored, 16)

            def step(c, ahead, ffn_b):
                if ahead:
                    move_qk(c + 1)
                if ffn_b:
                    store(c - 1)

            sp.dma_start(x_in[:, 0, :, :], x_chunks[0]).then_inc(x_first, 16)
            sp.dma_start(w1[:, :], W1).then_inc(w_loaded[W_W1], 16)
            sp.dma_start(wqkv_rows[:, :, :], w_qkv.rearrange("(s r) d -> r s d", s=3)).then_inc(w_loaded[W_QKV], 16)
            sp.dma_start(b2_bc[:, :], b2.rearrange("(a d) -> a d", a=1).broadcast_to([P, D])).then_inc(w_loaded[W_B2], 16)
            sp.dma_start(wout_rows[:, :], w_out).then_inc(w_loaded[W_OUT], 16)
            sp.dma_start(w2[:, :, :], W2.rearrange("(i p) d -> p i d", p=P)).then_inc(w_loaded[W_W2], 16)
            for r in range(0, ROWS, HD):
                sp.dma_start(proj_rows[r:r + HD, :, :], proj.rearrange("h d f -> d h f")).then_inc(w_loaded[W_PROJ], 16)
            sp.dma_start(x_in[:, 1:, :, :].rearrange("p c t d -> p (c t) d"), x_others).then_inc(x_rest, 16)
            sp.wait_ge(consts, 2)
            sp.dma_start(qk_packed[ROWS:ROWS + 1, :, :, :].bitcast(F32), ones[:, :]).then_inc(w_loaded[W_ONES], 16)
            sp.dma_start(proj_packed[ROWS:ROWS + 1, :, :].bitcast(F32), ones[0:HEADS * F // (HEADS * 2 * CHUNK // P), :]
                         ).then_inc(w_loaded[W_ONES], 16)
            sp.dma_start(bout_bc[:, :], b_out.rearrange("(a d) -> a d", a=1).broadcast_to([P, D])).then_inc(w_loaded[W_BOUT], 16)
            move_qk(0)
            schedule(sp, step)
            for g in range(2):
                sp.wait_ge(x3_ready, NC + g)
                sp.dma_start(out_chunks[NC - 1][:, TILES[g], :], x3[:, TILES[g], :]).then_inc(stored, 16)
            sp.wait_ge(stored, 16 * (NC + 1))

        @block.tensor
        def _(pe):
            def turn_normed(k, c, bank, tiles=slice(0, NT)):
                first = NT * c if k == 0 else 0
                for t in range(tiles.start, tiles.stop):
                    wait(pe, xn_ready[k], NT * c + t + 1)
                    mm = pe.transpose(bank[:, t * P:(t + 1) * P], xn[k][:, first + t, :], ident[:, :])
                mm.then_inc(turned[k], 1)

            def split_product(bank, w_hi, w_lo, k, tokens=slice(0, CHUNK)):
                pe.matmul(bank, w_hi, xnT_hi[k][:, tokens], start=True, stop=False)
                pe.matmul(bank, w_lo, xnT_hi[k][:, tokens], start=False, stop=False)
                return pe.matmul(bank, w_hi, xnT_lo[k][:, tokens], start=False, stop=True)

            def ffn_up(k, c, i, bank, tokens=None):
                cols = slice(i * P, (i + 1) * P)
                if tokens is None:
                    tokens = bass.ds(c * CHUNK, CHUNK) if k == 0 else slice(0, CHUNK)
                split_product(bank, w1_hi[:, cols], w1_lo[:, cols], 2 * k, tokens).then_inc(hidden_sum[k], 1)

            def ffn_down(k, call, i, bank, tiles=slice(0, NT)):
                wait(pe, hidden_ready[k], NI * call + i + 1)
                for t in range(tiles.start, tiles.stop):
                    mm = pe.matmul(bank[:, t * D:(t + 1) * D], hidden[k][:, i, t * P:(t + 1) * P], w2[:, i, :],
                                   start=(i == 0 and t == tiles.start),
                                   stop=(i == NI - 1 and t == tiles.stop - 1))
                if i == NI - 1:
                    mm.then_inc(y_sum[k], 1)

            def qk_product(tokens=slice(0, CHUNK)):
                for s in range(2):
                    mm = split_product(wide[0][:, s, tokens], wqk_hi[:, s, :], wqk_lo[:, s, :], 1, tokens)
                    if tokens.stop == CHUNK:
                        mm.then_inc(qk_sum, 1)

            def v_product():
                for t in range(NT):
                    bank, tokens = wide[1][:, 0, t * D:(t + 1) * D], slice(t * P, (t + 1) * P)
                    pe.matmul(bank, xnT_hi[1][:, tokens], wv_hi[:, :], start=True, stop=False)
                    pe.matmul(bank, xnT_hi[1][:, tokens], wv_lo[:, :], start=False, stop=False)
                    mm = pe.matmul(bank, xnT_lo[1][:, tokens], wv_hi[:, :], start=False, stop=True)
                mm.then_inc(v_sum, 1)

            def feature_product(c, h):
                for s in range(2):
                    mm = pe.matmul(wide[h % 2][:, s, :], proj_packed[:, h, :], qk_packed[:, h, s, :],
                                   start=True, stop=True)
                mm.then_inc(t_sum, 1)

            def first_features(c):
                wait(pe, qk_moved[0], 4 * 16 * (c + 1))
                feature_product(c, 0)
                wait(pe, v_ready, NB * (c + 1))
                feature_product(c, 1)

            def score(c, h):
                wait(pe, feat_ready, HEADS * c + h + 1)
                if h and h % GROUP == 0:
                    wait(pe, scores_out, NG * c + h // GROUP)
                for t in range(NT):
                    for j in range(NB):
                        tok = slice(t * P + j * BLOCK, t * P + (j + 1) * BLOCK)
                        col = ((h % GROUP) * NT + t) * BLOCK
                        mm = pe.matmul(S[j * BLOCK:(j + 1) * BLOCK, col:col + BLOCK],
                                       feat[:, h % FEAT_BUFS, 1, tok], feat[:, h % FEAT_BUFS, 0, tok],
                                       start=True, stop=True)
                mm.then_inc(scored, 1)

            def mix(c, g):
                wait(pe, scores_out, NG * c + g + 1)
                for hh in range(GROUP):
                    h = g * GROUP + hh
                    col = (h % HALF) * NB * VW
                    for t in range(NT):
                        mm = pe.matmul(O[t * BLOCK:(t + 1) * BLOCK, col:col + NB * VW],
                                       scores_sb[:, g % 2, hh, t, :],
                                       v_blocks[:, t, h, :, :].rearrange("p j w -> p (j w)"),
                                       start=True, stop=True)
                mm.then_inc(mixed, 1)

            def turn_attn(c, bank):
                wait(pe, attn_ready, 2 * c + 2)
                for j in range(NB):
                    mm = pe.transpose(bank[:, j * P:(j + 1) * P],
                                      attn[:, j, :, :].rearrange("p h d -> p (h d)"), ident[:, :])
                mm.then_inc(attn_turned, 1)

            def out_product(c, bank):
                wait(pe, attnT_ready, c + 1)
                for t in range(NT):
                    mm = pe.matmul(bank[:, t * D:(t + 1) * D],
                                   attnT[:, t, :, :].rearrange("p j q -> p (j q)"), woutT[:, :],
                                   start=True, stop=True)
                mm.then_inc(out_sum, 1)

            def step(c, ahead, ffn_b):
                if ahead:
                    wait(pe, xn_lo[0], c + 3)
                    ffn_up(0, c + 1, 0, X[0])
                    ffn_up(0, c + 1, 1, X[1])
                if ffn_b:
                    turn_normed(2, c - 1, O)
                if ahead:
                    wait(pe, hidden_ready[0], NI * (c + 2) + 1)
                    ffn_up(0, c + 1, 2, X[0])
                wait(pe, feat_ready, HEADS * c + 1)
                feature_product(c, 2)
                if ahead:
                    wait(pe, hidden_ready[0], NI * (c + 2) + 2)
                    ffn_up(0, c + 1, 3, X[1])
                else:
                    wait(pe, xn_lo[2], c)
                    ffn_up(1, c - 1, 0, X[0])
                    ffn_up(1, c - 1, 1, X[1])
                wait(pe, feat_ready, HEADS * c + 2)
                feature_product(c, 3)
                score(c, 0)
                score(c, 1)
                if ahead:
                    wait(pe, hidden_ready[0], NI * (c + 2) + 3)
                    ffn_down(0, c + 2, 0, X[0])
                    ffn_down(0, c + 2, 1, X[0])
                else:
                    wait(pe, hidden_ready[1], NI * (c - 1) + 1)
                    ffn_up(1, c - 1, 2, X[0])
                wait(pe, feat_ready, HEADS * c + 3)
                wait(pe, qk_moved[1], 4 * 16 * (c + 1))
                feature_product(c, 4)
                score(c, 2)
                if ahead:
                    ffn_down(0, c + 2, 2, X[0])
                    ffn_down(0, c + 2, 3, X[0])
                else:
                    wait(pe, hidden_ready[1], NI * (c - 1) + 2)
                    ffn_up(1, c - 1, 3, X[1])
                wait(pe, feat_ready, HEADS * c + 4)
                feature_product(c, 5)
                score(c, 3)
                if ffn_b:
                    wait(pe, xn_lo[2], c)
                mix(c, 0)
                if not ahead:
                    wait(pe, hidden_ready[1], NI * (c - 1) + 3)
                    ffn_down(1, c - 1, 0, X[0])
                wait(pe, feat_ready, HEADS * c + 5)
                feature_product(c, 6)
                score(c, 4)
                mix(c, 1)
                if ahead and ffn_b:
                    ffn_up(1, c - 1, 0, X[1])
                if not ahead:
                    ffn_down(1, c - 1, 1, X[0])
                wait(pe, feat_ready, HEADS * c + 6)
                feature_product(c, 7)
                score(c, 5)
                if ahead:
                    wait(pe, x1_ready, c + 3)
                    if ffn_b:
                        ffn_up(1, c - 1, 1, X[0])
                score(c, 6)
                if ahead:
                    if ffn_b:
                        wait(pe, hidden_ready[1], NI * (c - 1) + 1)
                    turn_normed(1, c + 1, X[1])
                    if ffn_b:
                        wait(pe, hidden_ready[1], NI * (c - 1) + 2)
                        ffn_up(1, c - 1, 2, X[0])
                score(c, 7)
                if ahead:
                    wait(pe, feat_ready, HEADS * c + 7)
                    wait(pe, xn_hi[1], c + 3)
                    wait(pe, xn_lo[1], c + 3)
                    qk_product()
                wait(pe, attn_ready, 2 * c + 1)
                mix(c, 2)
                mix(c, 3)
                if ahead and ffn_b:
                    ffn_up(1, c - 1, 3, X[1])
                    ffn_down(1, c - 1, 0, S)
                    wait(pe, hidden_ready[1], NI * (c - 1) + 3)
                turn_attn(c, X[0] if ahead else X[1])
                if ahead:
                    wait(pe, feat_ready, HEADS * c + 8)
                    v_product()
                out_product(c, O)
                if ahead:
                    first_features(c + 1)
                    if ffn_b:
                        for i in range(1, NI):
                            ffn_down(1, c - 1, i, S)
                else:
                    ffn_down(1, c - 1, 2, X[0])
                    ffn_down(1, c - 1, 3, X[0])

            pe.wait_ge(consts, 1)
            pe.wait_ge(w_loaded[W_B1], 16)
            pe.transpose(S[:, 0:NI], b1_rows[:, :], ident[0:NI, 0:NI]).then_inc(w_turned, 1)
            for g in range(2):
                turn_normed(0, 0, X[g], TILES[g])
            pe.wait_ge(w_loaded[W_QKV], 16)
            for s in range(3):
                pe.transpose(wide[1][:, 0, s * D:(s + 1) * D], wqkv_rows[:, s, :], ident[:, :])
            pe.wait_ge(w_loaded[W_OUT], 16)
            pe.transpose(wide[1][:, 0, 3 * D:4 * D], wout_rows[:, :], ident[:, :]).then_inc(w_turned, 1)
            pe.wait_ge(w_split, 1)
            pe.wait_ge(w_loaded[W_W2], 16)
            for g in range(2):
                wait(pe, xn_lo[0], g + 1)
                for i in range(NI):
                    if g == 1:
                        wait(pe, hidden_ready[0], i + 1)
                    ffn_up(0, 0, i, FIRST_SUM_BANKS[i][:, TOKENS[g]], TOKENS[g])
            for g in range(2):
                for i in range(NI):
                    ffn_down(0, g, i, X[g], TILES[g])
            for g in range(2):
                turn_normed(1, 0, FIRST_SUM_BANKS[g], TILES[g])
            pe.wait_ge(w_split, 8)
            for g in range(2):
                wait(pe, xn_hi[1], g + 1)
                wait(pe, xn_lo[1], g + 1)
                qk_product(TOKENS[g])
            v_product()
            for c in range(1, NC):
                turn_normed(0, c, FIRST_NORM_BANKS[c])
            pe.wait_ge(w_split, 9)
            pe.wait_ge(w_act, 4)
            pe.wait_ge(w_loaded[W_ONES], 32)
            pe.wait_ge(consts, 7)
            first_features(0)
            schedule(pe, step)
            for g in range(2):
                turn_normed(2, NC - 1, LAST_BANKS[g], TILES[g])
            for g in range(2):
                wait(pe, xn_lo[2], NC + g)
                for i in range(NI):
                    if g == 1:
                        wait(pe, hidden_ready[1], NI * (NC - 1) + i + 1)
                    ffn_up(1, NC - 1, i, LAST_SUM_BANKS[i][:, TOKENS[g]], TOKENS[g])
            for g in range(2):
                for i in range(NI):
                    ffn_down(1, NC - 1 + g, i, LAST_BANKS[g], TILES[g])

        @block.scalar
        def _(act):
            def normed_hi(k, call, bank, tokens=slice(0, CHUNK)):
                wait(act, turned[k], call + 1)
                nc.scalar.copy(xnT_hi[k][:, tokens], bank).then_inc(xn_hi[k], 1)

            def relu(k, call, i, bank, tokens=slice(0, CHUNK)):
                wait(act, hidden_sum[k], NI * call + i + 1)
                nc.scalar.activation(hidden[k][:, i, tokens], bank, ACT.Relu,
                                     bias=b1_cols[:, i:i + 1]).then_inc(hidden_ready[k], 1)

            def exp(c, h):
                wait(act, t_sum, HEADS * c + h + 1)
                wait(act, feat_ready, HEADS * c + h - 1)
                nc.scalar.activation(expo[:, h % 2, :, :], wide[h % 2][:, :, :], ACT.Exp,
                                     bias=minus_one[:, 0:1]).then_inc(exp_done, 1)

            def scores_copy(c, g):
                wait(act, scored, HEADS * c + GROUP * (g + 1))
                wait(act, mixed, NG * c + g - 1)
                nc.scalar.copy(scores_sb[:, g % 2, :, :, :].rearrange("p h t q -> p (h t q)"),
                               S[:, 0:GROUP * NT * BLOCK]).then_inc(scores_out, 1)

            def q_hi_copy(c):
                wait(act, qk_sum, 2 * c + 1)
                for g in range(2):
                    wait(act, qk_moved[g], 4 * 16 * c)
                nc.scalar.copy(qk_hi[:, 0, :], wide[0][:, 0, :]).then_inc(q_hi_ready, 1)

            def v_copy(c):
                wait(act, v_sum, c + 1)
                wait(act, mixed, NG * c)
                for j in range(NB):
                    rows = slice(j * BLOCK, (j + 1) * BLOCK)
                    nc.scalar.copy(v_blocks[rows, :, :, j, 0:HD].rearrange("p t h d -> p (t h) d"),
                                   wide[1][rows, 0, :].rearrange("p (th d) -> p th d", d=HD)).then_inc(v_ready, 1)

            def attn_copy(c, bank):
                wait(act, attn_turned, c + 1)
                wait(act, out_sum, c)
                nc.scalar.copy(attnT[:, :, :, :].rearrange("p t j q -> p j t q"),
                               bank.rearrange("p (j t q) -> p j t q", j=NB, t=NT)).then_inc(attnT_ready, 1)

            def step(c, ahead, ffn_b):
                if ahead:
                    relu(0, c + 2, 0, X[0])
                    relu(0, c + 2, 1, X[1])
                if ffn_b:
                    normed_hi(2, c - 1, O)
                exp(c, 2)
                if ahead:
                    relu(0, c + 2, 2, X[0])
                else:
                    relu(1, c - 1, 0, X[0])
                exp(c, 3)
                if ahead:
                    relu(0, c + 2, 3, X[1])
                else:
                    relu(1, c - 1, 1, X[1])
                scores_copy(c, 0)
                exp(c, 4)
                if not ahead:
                    relu(1, c - 1, 2, X[0])
                exp(c, 5)
                if not ahead:
                    relu(1, c - 1, 3, X[1])
                scores_copy(c, 1)
                exp(c, 6)
                if ahead and ffn_b:
                    relu(1, c - 1, 0, X[1])
                exp(c, 7)
                scores_copy(c, 2)
                if ahead:
                    if ffn_b:
                        relu(1, c - 1, 1, X[0])
                    normed_hi(1, c + 2, X[1])
                    if ffn_b:
                        relu(1, c - 1, 2, X[0])
                scores_copy(c, 3)
                if ahead:
                    q_hi_copy(c + 1)
                    if ffn_b:
                        relu(1, c - 1, 3, X[1])
                attn_copy(c, X[0] if ahead else X[1])
                if ahead:
                    v_copy(c + 1)
                    exp(c + 1, 0)
                    exp(c + 1, 1)

            act.dma_start(b1_rows[:, :], b1.rearrange("(i p) -> i p", p=P)).then_inc(w_loaded[W_B1], 16)
            act.wait_ge(pool_set, 1)
            nc.scalar.mul(minus_one[:, :], minus_half[:, 0:1], 2.0).then_inc(w_act, 1)
            act.wait_ge(w_loaded[W_W1], 16)
            nc.scalar.copy(w1_hi[:, :], w1[:, :]).then_inc(w1_hi_ready, 1)
            act.wait_ge(w_turned, 1)
            nc.scalar.copy(b1_cols[:, :], S[:, 0:NI]).then_inc(w_act, 1)
            for g in range(2):
                normed_hi(0, g, X[g][:, TOKENS[g]], TOKENS[g])
            act.wait_ge(w_act, 2)
            for g in range(2):
                for i in range(NI):
                    relu(0, g, i, FIRST_SUM_BANKS[i][:, TOKENS[g]], TOKENS[g])
            act.wait_ge(w_loaded[W_PROJ], 16 * 4)
            nc.scalar.copy(proj_round[:, :, :], proj_rows[:, :, :]).then_inc(w_act, 1)
            nc.scalar.copy(proj_packed[0:2 * HD, :, :], proj_rows[0:2 * HD, :, :]).then_inc(w_act, 1)
            for g in range(2):
                normed_hi(1, g, FIRST_SUM_BANKS[g][:, TOKENS[g]], TOKENS[g])
            q_hi_copy(0)
            act.wait_ge(consts, 7)
            v_copy(0)
            for c in range(1, NC):
                normed_hi(0, c + 1, FIRST_NORM_BANKS[c], slice(c * CHUNK, (c + 1) * CHUNK))
            exp(0, 0)
            exp(0, 1)
            schedule(act, step)
            for g in range(2):
                normed_hi(2, NC - 1 + g, LAST_BANKS[g][:, TOKENS[g]], TOKENS[g])
            for g in range(2):
                for i in range(NI):
                    relu(1, NC - 1 + g, i, LAST_SUM_BANKS[i][:, TOKENS[g]], TOKENS[g])

        @block.vector
        def _(dve):
            def norm_stats(k, n, src, tiles=slice(0, NT)):
                norm_parts(k, src, tiles)
                norm_join(k, n, tiles)

            def norm_parts(k, src, tiles):
                for t in range(tiles.stop - tiles.start):
                    bn = nc.vector.bn_stats(stats[k][:, tiles.start + t, :], src[:, t, :])
                bn.then_inc(stat_part[k], 1)

            def norm_join(k, n, tiles):
                base = 4 * n
                even, odd = stats[k][:, tiles, 0:3], stats[k][:, tiles, 3:6]
                wait(dve, stat_part[k], base + 1)
                nc.vector.tensor_tensor(gap[k][:, tiles], even[:, :, 1], odd[:, :, 1], ALU.subtract)
                nc.vector.tensor_tensor(both[k][:, tiles, :], even[:, :, 1:3], odd[:, :, 1:3], ALU.add).then_inc(stat_part[k], 1)
                wait(dve, stat_part[k], base + 2)
                nc.vector.tensor_tensor(gap_sq[k][:, tiles], gap[k][:, tiles], gap[k][:, tiles], ALU.mult)
                nc.vector.tensor_scalar(mean[k][:, tiles], both[k][:, tiles, 0], 0.5, None, ALU.mult)
                nc.vector.tensor_scalar(spread[k][:, tiles], both[k][:, tiles, 1], 1.0 / D, EPS, ALU.mult, ALU.add).then_inc(stat_part[k], 1)
                wait(dve, stat_part[k], base + 3)
                nc.vector.scalar_tensor_tensor(out=var_eps[k][:, tiles], in0=gap_sq[k][:, tiles], scalar=0.25,
                                               in1=spread[k][:, tiles], op0=ALU.mult, op1=ALU.add).then_inc(stat_part[k], 1)

            def norm_apply(k, src, tiles=slice(0, NT)):
                for t in range(tiles.start, tiles.stop):
                    nc.vector.tensor_scalar(xn[k][:, t, :], src[:, t - tiles.start, :], mean[k][:, t:t + 1],
                                            rstd[k][:, t:t + 1], ALU.subtract, ALU.mult).then_inc(xn_ready[k], 1)

            def normed_lo(k, call, bank, tokens=slice(0, CHUNK)):
                wait(dve, xn_hi[k], call + 1)
                nc.vector.tensor_tensor(xnT_lo[k][:, tokens], bank, xnT_hi[k][:, tokens].bitcast(F32),
                                        ALU.subtract).then_inc(xn_lo[k], 1)

            def feature(c, h):
                wait(dve, exp_done, HEADS * c + h + 1)
                wait(dve, scored, HEADS * c + h + 1 - FEAT_BUFS if h >= FEAT_BUFS else HEADS * c)
                nc.vector.scalar_tensor_tensor(
                    out=feat[:, h % FEAT_BUFS, :, :], in0=expo[:, h % 2, :, :], scalar=1.0,
                    in1=wide[h % 2][:, :, :], op0=ALU.min, op1=ALU.max).then_inc(feat_ready, 1)

            def divide(c, half):
                n = HALF
                sums = O[:, 0:n * NB * VW].rearrange("p (h j w) -> p h j w", h=n, j=NB)
                wait(dve, mixed, NG * c + 2 * (half + 1))
                nc.vector.tensor_scalar(z[:, half, :, :], sums[:, :, :, HD], Z_EPS, None,
                                        ALU.add).then_inc(z_part, 1)
                wait(dve, z_part, 4 * c + 2 * half + 1)
                nc.vector.reciprocal(z_inv[:, half, :, :], z[:, half, :, :]).then_inc(z_part, 1)
                wait(dve, z_part, 4 * c + 2 * half + 2)
                wait(dve, attn_turned, c)
                nc.vector.tensor_tensor(
                    attn[:, :, n * half:n * (half + 1), :].rearrange("p j h d -> p h j d"),
                    sums[:, :, :, 0:HD],
                    z_inv[:, half, :, :].rearrange("p h (j a) -> p h j a", a=1).broadcast_to([P, n, NB, HD]),
                    ALU.mult).then_inc(attn_ready, 1)

            def step(c, ahead, ffn_b):
                feature(c, 1)
                if ffn_b:
                    normed_lo(2, c - 1, O)
                for h in range(2, 6):
                    feature(c, h)
                if ahead:
                    ffn_a_residual(c + 1)
                    norm_stats(1, c + 2, x1)
                feature(c, 6)
                if ahead:
                    wait(dve, rstd_ready[1], c + 3)
                    norm_apply(1, x1)
                else:
                    divide(c, 0)
                feature(c, 7)
                if ahead:
                    normed_lo(1, c + 2, X[1])
                    divide(c, 0)
                    qk_parts(c + 1)
                divide(c, 1)
                attn_residual(c, ffn_b)
                if ahead:
                    feature(c + 1, 0)
                    wait(dve, rstd_ready[2], c + 1)
                    norm_apply(2, x2)
                    if ffn_b:
                        ffn_b_residual(c - 1, S)

            def attn_residual(c, ffn_b):
                wait(dve, out_sum, c + 1)
                wait(dve, x1_bout_ready, c + 1)
                if ffn_b:
                    wait(dve, x2_b2_ready, c)
                nc.vector.tensor_tensor(x2[:, :, :], x1_bout[:, :, :], O.rearrange("p (t d) -> p t d", d=D),
                                        ALU.add).then_inc(x2_ready, 1)
                wait(dve, x2_ready, c + 1)
                norm_stats(2, c, x2)

            def ffn_a_residual(c):
                wait(dve, y_sum[0], c + 2)
                wait(dve, x1_bout_ready, c)
                add_half(x1, x_b2[:, c, :, :], X[0], x1_ready)
                wait(dve, x1_ready, c + 2)

            def ffn_b_residual(c, bank):
                wait(dve, y_sum[1], c + 1)
                wait(dve, x2_b2_ready, c + 1)
                wait(dve, stored, 16 * c)
                add_half(x3, x2_b2, bank, x3_ready)

            def add_half(dst, src, bank, ready, tiles=slice(0, NT)):
                nc.vector.scalar_tensor_tensor(out=dst[:, tiles, :],
                                               in0=bank.rearrange("p (t d) -> p t d", d=D)[:, tiles, :],
                                               scalar=0.5, in1=src[:, tiles, :], op0=ALU.mult,
                                               op1=ALU.add).then_inc(ready, 1)

            def qk_parts(c):
                wait(dve, qk_sum, 2 * c + 2)
                for g in range(2):
                    wait(dve, qk_moved[g], 4 * 16 * c)
                nc.vector.tensor_copy(qk_hi[:, 1, :], wide[0][:, 1, :]).then_inc(k_hi_ready, 1)
                for s, ready in ((0, q_hi_ready), (1, k_hi_ready)):
                    wait(dve, ready, c + 1)
                    nc.vector.tensor_tensor(qk_lo[:, s, :], wide[0][:, s, :], qk_hi[:, s, :].bitcast(F32),
                                            ALU.subtract).then_inc(qk_lo_ready, 1)

            dve.wait_ge(x_first, 16)
            norm_stats(0, 0, x_in[:, 0, :, :])
            dve.wait_ge(w1_hi_ready, 1)
            nc.vector.tensor_tensor(w1_lo[:, :], w1[:, :], w1_hi[:, :].bitcast(F32), ALU.subtract).then_inc(w_split, 1)
            for g in range(2):
                dve.wait_ge(rstd_ready[0], g + 1)
                norm_apply(0, x_in[:, 0, TILES[g], :], TILES[g])
            for g in range(2):
                normed_lo(0, g, X[g][:, TOKENS[g]], TOKENS[g])
            dve.wait_ge(w_turned, 2)
            turned_w = wide[1][:, 0, :].rearrange("p (s c) -> p s c", c=D)
            for s in range(2):
                nc.vector.tensor_copy(wqk_hi[:, s, :].rearrange("p (g d h) -> p g d h", g=2, h=HALF),
                                      turned_w[:, s, :].rearrange("p (g h d) -> p g d h", g=2, h=HALF)).then_inc(w_split, 1)
            nc.vector.tensor_copy(wv_hi[:, :], turned_w[:, 2, :]).then_inc(w_split, 1)
            dve.wait_ge(w_split, 4)
            for s in range(2):
                nc.vector.tensor_tensor(wqk_lo[:, s, :].rearrange("p (g d h) -> p g d h", g=2, h=HALF),
                                        turned_w[:, s, :].rearrange("p (g h d) -> p g d h", g=2, h=HALF),
                                        wqk_hi[:, s, :].rearrange("p (g d h) -> p g d h", g=2, h=HALF).bitcast(F32),
                                        ALU.subtract).then_inc(w_split, 1)
            nc.vector.tensor_tensor(wv_lo[:, :], turned_w[:, 2, :], wv_hi[:, :].bitcast(F32),
                                    ALU.subtract).then_inc(w_split, 1)
            nc.vector.tensor_copy(woutT[:, :], turned_w[:, 3, :]).then_inc(w_split, 1)
            dve.wait_ge(x_rest, 16)
            others, x_in_others = slice(NT, NC * NT), x_in[:, 1:, :, :].rearrange("p c t d -> p (c t) d")
            norm_stats(0, 1, x_in_others, others)
            dve.wait_ge(x_b2_ready, 2)
            for g in range(2):
                dve.wait_ge(y_sum[0], g + 1)
                add_half(x1, x_b2[:, 0, :, :], X[g], x1_ready, TILES[g])
                dve.wait_ge(x1_ready, g + 1)
                norm_parts(1, x1[:, TILES[g], :], TILES[g])
                if g == 1:
                    dve.wait_ge(rstd_ready[1], 1)
                    norm_apply(1, x1[:, TILES[0], :], TILES[0])
                norm_join(1, g, TILES[g])
            dve.wait_ge(rstd_ready[1], 2)
            norm_apply(1, x1[:, TILES[1], :], TILES[1])
            for g in range(2):
                normed_lo(1, g, FIRST_SUM_BANKS[g][:, TOKENS[g]], TOKENS[g])
            dve.wait_ge(w_act, 3)
            nc.vector.tensor_tensor(proj_packed[2 * HD:ROWS, :, :], proj_rows[2 * HD:ROWS, :, :],
                                    proj_round[2 * HD:ROWS, :, :].bitcast(F32), ALU.subtract).then_inc(w_split, 1)
            dve.wait_ge(rstd_ready[0], 3)
            norm_apply(0, x_in[:, 1, :, :], slice(NT, 2 * NT))
            qk_parts(0)
            norm_apply(0, x_in[:, 2:, :, :].rearrange("p c t d -> p (c t) d"), slice(2 * NT, NC * NT))
            for c in range(1, NC):
                normed_lo(0, c + 1, FIRST_NORM_BANKS[c], slice(c * CHUNK, (c + 1) * CHUNK))
            dve.wait_ge(x_b2_ready, NC + 1)
            feature(0, 0)
            schedule(dve, step)
            for g in range(2):
                dve.wait_ge(rstd_ready[2], NC + g)
                norm_apply(2, x2[:, TILES[g], :], TILES[g])
            for g in range(2):
                normed_lo(2, NC - 1 + g, LAST_BANKS[g][:, TOKENS[g]], TOKENS[g])
            ffn_b_residual(NC - 2, X[0])
            dve.wait_ge(x2_b2_ready, NC)
            dve.wait_ge(stored, 16 * (NC - 1))
            for g in range(2):
                dve.wait_ge(y_sum[1], NC + g)
                add_half(x3, x2_b2, LAST_BANKS[g], x3_ready, TILES[g])

        @block.gpsimd
        def _(pool):
            def reciprocal_root(k, tiles=slice(0, NT)):
                nc.gpsimd.tensor_tensor(rstd[k][:, tiles], var_eps[k][:, tiles], minus_half[:, tiles], ALU.pow).then_inc(rstd_ready[k], 1)

            def add_bout(c):
                wait(pool, x1_ready, c + 2)
                wait(pool, x2_ready, c)
                nc.gpsimd.tensor_tensor(x1_bout[:, :, :], x1[:, :, :],
                                        bout_bc[:, :].rearrange("p (a d) -> p a d", a=1).broadcast_to([P, NT, D]),
                                        ALU.add).then_inc(x1_bout_ready, 1)

            def add_b2(c):
                nc.gpsimd.tensor_tensor(x2_b2[:, :, :], x2[:, :, :],
                                        b2_half[:, :].rearrange("p (a d) -> p a d", a=1).broadcast_to([P, NT, D]),
                                        ALU.add).then_inc(x2_b2_ready, 1)

            def step(c, ahead, ffn_b):
                if ffn_b:
                    add_b2(c - 1)
                if ahead:
                    wait(pool, stat_part[1], 4 * (c + 3))
                    reciprocal_root(1)
                    wait(pool, stat_part[2], 4 * (c + 1))
                    reciprocal_root(2)
                    add_bout(c + 1)
                    if ffn_b:
                        wait(pool, x3_ready, c)

            nc.gpsimd.memset(minus_half[:, :], -0.5).then_inc(pool_set, 1)
            nc.gpsimd.memset(ident[:, :], 0.0).then_inc(pool_set, 1)
            pool.wait_ge(pool_set, 2)
            nc.gpsimd.affine_select(out=ident[:, :], in_=ident[:, :], compare_op=ALU.not_equal, fill=1.0,
                                    base=0, pattern=[[-1, P]], channel_multiplier=1).then_inc(consts, 1)
            nc.gpsimd.memset(ones[:, :], 1.0).then_inc(consts, 1)
            pool.wait_ge(stat_part[0], 4)
            for g in range(2):
                reciprocal_root(0, TILES[g])

            def add_b2_to_x(c):
                nc.gpsimd.tensor_tensor(x_b2[:, c, :, :], x_in[:, c, :, :],
                                        b2_half[:, :].rearrange("p (a d) -> p a d", a=1).broadcast_to([P, NT, D]),
                                        ALU.add).then_inc(x_b2_ready, 1)

            pool.wait_ge(w_loaded[W_B2], 16)
            nc.gpsimd.tensor_scalar(b2_half[:, :], b2_bc[:, :], 0.5, None, ALU.mult).then_inc(x_b2_ready, 1)
            pool.wait_ge(x_b2_ready, 1)
            pool.wait_ge(x_first, 16)
            add_b2_to_x(0)
            nc.gpsimd.memset(v_blocks[:, :, :, :, :], 0.0).then_inc(consts, 1)
            pool.wait_ge(consts, 3)
            for j in range(NB):
                nc.gpsimd.memset(v_blocks[j * BLOCK:(j + 1) * BLOCK, :, :, j, HD:VW], 1.0).then_inc(consts, 1)
                pool.wait_ge(consts, 4 + j)
            for g in range(2):
                pool.wait_ge(stat_part[1], 4 * (g + 1))
                reciprocal_root(1, TILES[g])
            pool.wait_ge(stat_part[0], 8)
            reciprocal_root(0, slice(NT, NC * NT))
            pool.wait_ge(x_rest, 16)
            for c in range(1, NC):
                add_b2_to_x(c)
            pool.wait_ge(w_loaded[W_BOUT], 16)
            add_bout(0)
            schedule(pool, step)
            pool.wait_ge(stat_part[2], 4 * NC)
            for g in range(2):
                reciprocal_root(2, TILES[g])
            pool.wait_ge(x3_ready, NC - 1)
            add_b2(NC - 1)


_INS = ['L0_attn_x', 'L0_attn_w_qkv', 'L0_attn_w_out', 'L0_attn_b_out', 'L0_attn_proj',
        'L0_ffn_W1', 'L0_ffn_b1', 'L0_ffn_W2', 'L0_ffn_b2']


def kernel(**inputs):
    import numpy as _np
    import concourse.bacc as _bacc
    from concourse import mybir as _mybir
    from concourse.bass_utils import run_bass_kernel_spmd as _run

    nc = _bacc.Bacc("TRN2", target_bir_lowering=False, num_devices=1)
    arrays, args = {}, []
    for name in _INS:
        a = _np.ascontiguousarray(inputs[name])
        arrays[f"in_{name}_dram"] = a
        args.append(nc.dram_tensor(f"in_{name}_dram", a.shape, _mybir.dt.from_np(a.dtype), kind="ExternalInput").ap())
    shape = inputs['L0_attn_x'].shape
    args.append(nc.dram_tensor("out_0_dram", shape, _mybir.dt.from_np(_np.dtype("float32")), kind="ExternalOutput").ap())
    macaron_kernel(nc, *args)
    r = _run(nc, [arrays], core_ids=[0])
    return r.results[0]["out_0_dram"]
```
